# Optimizing a Trainium2 kernel written in Bass

```python
import numpy as np
import jax
import jax.numpy as jnp

def _softmax(x, axis=-1):
    return jax.nn.softmax(x, axis=axis)

def _gelu(x):
    return jax.nn.gelu(x, approximate=True)

def _silu(x):
    return jax.nn.silu(x)

def _sigmoid(x):
    return jax.nn.sigmoid(x)

def _layernorm(x, axis=-1, eps=1e-05):
    m = jnp.mean(x, axis=axis, keepdims=True)
    v = jnp.var(x, axis=axis, keepdims=True)
    return (x - m) / jnp.sqrt(v + eps)

def _scatter_add(tgt, idx, src, axis=0):
    return tgt.at[idx].add(src)

def _segment_sum(src, seg, n):
    return jax.ops.segment_sum(src, seg, n)
kernel_name = 'mk_prb_d1_jaxref_r8_ff5d57'

def setup_inputs(seed: int=0):
    np.random.seed(seed)
    _w = jnp.asarray

    def _L0_attn_setup():
        import jax, jax.numpy as jnp
        import numpy as np
        N_HEAD = 16
        N_EMBD = 128
        CHUNK = 64
        ROPE_BASE = 10000.0

        def _rope_tables(head_dim, chunk_size, dtype):
            inv_freq = 1.0 / ROPE_BASE ** (jnp.arange(0, head_dim, 2, dtype=jnp.float32) / head_dim)
            t = jnp.arange(chunk_size, dtype=jnp.float32)
            freqs = jnp.outer(t, inv_freq)
            return (jnp.cos(freqs).astype(dtype), jnp.sin(freqs).astype(dtype))

        def _apply_rope(x, cos, sin):
            d = x.shape[-1] // 2
            x1, x2 = (x[..., :d], x[..., d:])
            c = cos[None, None, :, None, :]
            s = sin[None, None, :, None, :]
            return jnp.concatenate([x1 * c + x2 * s, -x1 * s + x2 * c], axis=-1)
        key = jax.random.key(seed)
        k1, k2, k3 = jax.random.split(key, 3)
        B, T, C = (4, 512, N_EMBD)
        x = jax.random.normal(k1, (B, T, C), dtype=jnp.float32)
        w_attn = jax.random.normal(k2, (3 * C, C), dtype=jnp.float32) / np.sqrt(C)
        w_proj = jax.random.normal(k3, (C, C), dtype=jnp.float32) / np.sqrt(C)
        return {'x': x, 'w_attn': w_attn, 'w_proj': w_proj}
    _L0_attn_in = _L0_attn_setup()

    def _L0_ffn_setup():
        import jax, jax.numpy as jnp
        import numpy as np
        from jax import lax
        D = 128
        E = 8
        F = 512
        TOP_K = 2
        key = jax.random.key(seed)
        ks = jax.random.split(key, 8)
        s = 0.02
        return {'x': jax.random.normal(ks[0], (4, 256, D), dtype=jnp.float32), 'gate_w': jax.random.normal(ks[1], (D, E), dtype=jnp.float32) * s, 'gate_b': jnp.zeros((E,), dtype=jnp.float32), 'w1': jax.random.normal(ks[2], (E, D, F), dtype=jnp.float32) * s, 'b1': jnp.zeros((E, F), dtype=jnp.float32), 'w2': jax.random.normal(ks[3], (E, F, D), dtype=jnp.float32) * s, 'b2': jnp.zeros((E, D), dtype=jnp.float32)}
    _L0_ffn_in = _L0_ffn_setup()
    _d = {'L0_attn_x': _L0_attn_in['x'], 'L0_attn_w_attn': _L0_attn_in['w_attn'], 'L0_attn_w_proj': _L0_attn_in['w_proj'], 'L0_ffn_gate_w': _L0_ffn_in['gate_w'], 'L0_ffn_gate_b': _L0_ffn_in['gate_b'], 'L0_ffn_w1': _L0_ffn_in['w1'], 'L0_ffn_b1': _L0_ffn_in['b1'], 'L0_ffn_w2': _L0_ffn_in['w2'], 'L0_ffn_b2': _L0_ffn_in['b2']}
    _x0 = _d['L0_attn_x']
    _d['L0_attn_x'] = jax.random.normal(jax.random.fold_in(jax.random.key(seed), 1), (2, 2048, 128), dtype=_x0.dtype)
    del _x0
    return _d

def reference(L0_attn_x, L0_attn_w_attn, L0_attn_w_proj, L0_ffn_gate_w, L0_ffn_gate_b, L0_ffn_w1, L0_ffn_b1, L0_ffn_w2, L0_ffn_b2):

    def _L0_attn_ref(x, w_attn, w_proj):
        import jax, jax.numpy as jnp
        import numpy as np
        N_HEAD = 16
        N_EMBD = 128
        CHUNK = 64
        ROPE_BASE = 10000.0

        def _rope_tables(head_dim, chunk_size, dtype):
            inv_freq = 1.0 / ROPE_BASE ** (jnp.arange(0, head_dim, 2, dtype=jnp.float32) / head_dim)
            t = jnp.arange(chunk_size, dtype=jnp.float32)
            freqs = jnp.outer(t, inv_freq)
            return (jnp.cos(freqs).astype(dtype), jnp.sin(freqs).astype(dtype))

        def _apply_rope(x, cos, sin):
            d = x.shape[-1] // 2
            x1, x2 = (x[..., :d], x[..., d:])
            c = cos[None, None, :, None, :]
            s = sin[None, None, :, None, :]
            return jnp.concatenate([x1 * c + x2 * s, -x1 * s + x2 * c], axis=-1)
        B, T, C = x.shape
        H, cs = (N_HEAD, CHUNK)
        d = C // H
        nc = T // cs
        qkv = jnp.einsum('btc,fc->btf', x, w_attn)
        q, k, v = jnp.split(qkv, 3, axis=2)
        q = q.reshape(B, nc, cs, H, d)
        k = k.reshape(B, nc, cs, H, d)
        v = v.reshape(B, nc, cs, H, d)
        cos, sin = _rope_tables(d, cs, x.dtype)
        q = _apply_rope(q, cos, sin)
        k = _apply_rope(k, cos, sin)
        scale = 1.0 / np.sqrt(d)
        scores = jnp.einsum('bnqhd,bnkhd->bnhqk', q, k) * scale
        p = jax.nn.softmax(scores, axis=-1)
        y = jnp.einsum('bnhqk,bnkhd->bnqhd', p, v)
        y = y.reshape(B, T, C)
        return jnp.einsum('btc,oc->bto', y, w_proj)

    def _L0_ffn_ref(x, gate_w, gate_b, w1, b1, w2, b2):
        import jax, jax.numpy as jnp
        import numpy as np
        from jax import lax
        D = 128
        E = 8
        F = 512
        TOP_K = 2
        B, S, _ = x.shape
        flat = x.reshape(-1, D)
        T = flat.shape[0]
        logits = flat @ gate_w + gate_b
        topv, topi = lax.top_k(logits, TOP_K)
        topw = jax.nn.softmax(topv.astype(jnp.float32), axis=-1).astype(x.dtype)
        routing = jnp.zeros_like(logits).at[jnp.arange(T)[:, None], topi].set(topw)

        def body(acc, params):
            W1e, b1e, W2e, b2e, we = params
            h = jax.nn.gelu(flat @ W1e + b1e, approximate=False)
            out = h @ W2e + b2e
            return (acc + out * we[:, None], None)
        init = jnp.zeros_like(flat)
        final, _ = lax.scan(body, init, (w1, b1, w2, b2, routing.T))
        return final.reshape(B, S, D)
    x = L0_attn_x
    xn = _layernorm(x, axis=-1)
    x = x + _L0_attn_ref(xn, L0_attn_w_attn, L0_attn_w_proj) + _L0_ffn_ref(xn, L0_ffn_gate_w, L0_ffn_gate_b, L0_ffn_w1, L0_ffn_b1, L0_ffn_w2, L0_ffn_b2)
    return x

_drawn_inputs = setup_inputs


def setup_inputs(seed=0):
    import zlib

    import numpy as np

    out = dict(_drawn_inputs(seed))
    spreads = {'L0_ffn_gate_b': (0.0, 0.1), 'L0_ffn_b1': (0.0, 0.492), 'L0_ffn_b2': (0.0, 0.1)}
    factors = {}
    for name, (base, spread) in spreads.items():
        noise = np.random.default_rng([zlib.crc32(name.encode()), seed]).standard_normal(out[name].shape)
        drawn = base * np.exp(spread * noise) if base else spread * noise
        out[name] = jnp.asarray(drawn.astype(out[name].dtype))
    for name, factor in factors.items():
        out[name] = (out[name] * factor).astype(out[name].dtype)
    return out
```

```python
from contextlib import ExitStack

import numpy as np

import concourse.bass as bass
from concourse import mybir

F32 = mybir.dt.float32
I32 = mybir.dt.int32
ALU = mybir.AluOpType
ACT = mybir.ActivationFunctionType
AX = mybir.AxisListType

P = 128
BATCH, SEQ, C = 2, 2048, 128
TOKENS = BATCH * SEQ
TILES = TOKENS // P
HALF = TILES // 2
HEADS, CHUNK = 16, 64
HD = C // HEADS
NJ, NG = 4, 4
GRP = NJ * HD
DIAG = 2 * GRP + HD
SCALE = 1.0 / float(np.sqrt(HD))
ROPE_BASE = 10000.0
EPS = 1e-5
E, F, TOP_K = 8, 512, 2
FC = F // P
SLOT_TILES = TOKENS * TOP_K // P + E
SLOTS = SLOT_TILES * P
FAR = -3.0e38

K_ID, K_COS, K_SIN, K_MASK = 0, P, P + CHUNK, P + 2 * CHUNK
K_TRI = K_MASK + NJ
K_ONE = K_TRI + P
K_E8 = K_ONE + P
K_STEP = K_E8 + E
K_START = K_STEP + TILES
K_ALL = K_START + SLOT_TILES

W_B1, W_2, W_B2 = F, F + FC, F + FC + FC * C
W_ALL = W_B2 + C


def constants():
    k = np.zeros((P, K_ALL), np.float32)
    k[:, K_ID:K_ID + P] = np.eye(P)
    row = np.arange(P)
    d = row % HD
    freq = (np.float32(1.0) / np.float32(ROPE_BASE) ** (np.arange(0, HD, 2, dtype=np.float32) / np.float32(HD))).astype(np.float32)
    angle = np.outer(freq[d % (HD // 2)], np.arange(CHUNK, dtype=np.float32)).astype(np.float32)
    k[:, K_COS:K_COS + CHUNK] = np.cos(angle)
    k[:, K_SIN:K_SIN + CHUNK] = np.sin(angle) * np.where(d < HD // 2, 1.0, -1.0)[:, None]
    for j in range(NJ):
        k[:, K_MASK + j] = (row // HD) % NJ == j
    k[:, K_TRI:K_TRI + P] = row[:, None] < row[None, :]
    k[:, K_ONE:K_ONE + P] = 1.0
    k[:, K_E8:K_E8 + E] = np.arange(E) - E
    k[:, K_STEP:K_STEP + TILES] = np.arange(TILES) * P
    k[:, K_START:K_START + SLOT_TILES] = np.arange(SLOT_TILES) * P
    return k


def build(nc, x, w_attn, w_proj, gate_w, gate_b, w1, b1, w2, b2, consts, out):
    with ExitStack() as ctx:
        def sb(name, shape, dt=F32):
            return ctx.enter_context(nc.sbuf_tensor("sb_" + name, shape, dt))

        def sem(name):
            return ctx.enter_context(nc.semaphore(name))

        xg_dram = nc.dram_tensor("slot_rows", [SLOTS, C], F32).ap()
        yg_dram = nc.dram_tensor("slot_results", [SLOTS, C], F32).ap()

        kc = sb("consts", [P, K_ALL])
        acc = sb("acc", [P, TILES, C])
        xn = sb("xn", [P, TILES, C])
        xnT = sb("xnT", [P, TOKENS])
        wall = sb("expert_weights", [P, E, W_ALL])
        wqk = sb("wqk", [P, 4, P])
        wv = sb("wv", [P, P])
        wp = sb("wp", [P, P])
        raw = sb("raw_weights", [P, 5, P])
        wgate = sb("wgate", [P, P])
        gbias = sb("gbias", [P, E])
        zeros = sb("zeros", [P, P])
        mask = sb("mask", [P, NJ, P])

        stats = sb("stats", [P, TILES, 6])
        mv = sb("mv", [P, TILES, 2])
        var = sb("var", [P, TILES])
        power = sb("power", [P, TILES])
        rstd = sb("rstd", [P, TILES])
        xr = sb("xr", [P, 2, P])

        lg = sb("logits", [P, TILES, E])
        best = sb("best", [P, 2, TILES])
        pick = sb("pick", [P, 2, TILES])
        work = sb("work", [P, TILES, E])
        hot = sb("hot", [P, 2, TILES, E])
        both = sb("both", [P, E, TILES])
        run = sb("run", [P, E * TILES])
        place = sb("place", [P, E, TILES])
        load_e = sb("load_e", [P, E])
        many = sb("many", [P, E, TILES])
        padded = sb("padded", [P, E])
        ends = sb("ends", [P, E])
        shift = sb("shift", [P, E])
        posf = sb("posf", [P, 2, TILES])
        pos = sb("pos", [P, 2, TILES], I32)
        late = sb("late", [1, SLOT_TILES, E])
        eidf = sb("eidf", [1, SLOT_TILES])
        eid = sb("eid", [1, SLOT_TILES], I32)
        gap = sb("gap", [P, TILES])
        den = sb("den", [P, TILES])
        wt = sb("wt", [P, 2, TILES])

        rp = sb("rope_products", [P, 4, P])
        rot = sb("rot", [P, 2, P])
        qm = sb("qm", [P, 2, NJ, P])
        kz = sb("kz", [P, 2, NG, P])
        xv = sb("xv", [P, 2, 2, 2, CHUNK])
        vbd = sb("vbd", [P, 2, 2, 2, NJ * DIAG])
        pr = sb("probs", [P, 2, NJ * NG, CHUNK])
        pT = sb("probsT", [P, 2, NJ * 2, P])
        mx = sb("mx", [P, NJ * NG])
        sm = sb("sm", [P, NJ * NG])
        rc = sb("rc", [P, NJ * NG])
        rexp = sb("rexp", [P, NG, NJ, HD])
        rT = sb("rT", [P, P])
        yT = sb("yT", [P, 2, P])

        xs = sb("xs", [P, 2, P])
        xsT = sb("xsT", [P, 2, P])
        wl1 = sb("wl1", [P, 2, W_2])
        wl2 = sb("wl2", [P, 2, W_ALL - W_2])
        hT = sb("hT", [P, 2, FC, P])
        ys = sb("ys", [P, 2, P])
        got = sb("got", [P, 2, TILES, C])

        qk_ps = ctx.enter_context(nc.psum_tensor("qk_ps", [P, 4, P], F32))
        v_ps = ctx.enter_context(nc.psum_tensor("v_ps", [P, 4, P], F32))
        s_ps = ctx.enter_context(nc.psum_tensor("s_ps", [P, NJ * NG, CHUNK], F32))
        t_ps = ctx.enter_context(nc.psum_tensor("t_ps", [P, 8, P], F32))
        y_ps = ctx.enter_context(nc.psum_tensor("y_ps", [P, 4, P], F32))
        m_ps = ctx.enter_context(nc.psum_tensor("m_ps", [P, 4, P], F32))

        x_in = [sem(f"x_in{i}") for i in range(4)]
        consts_in, wraw_in, gate_in, wall_in = sem("consts_in"), sem("wraw_in"), sem("gate_in"), sem("wall_in")
        fills, wgate_ready, wT_done, wT_copied, mask_ready = (
            sem("fills"), sem("wgate_ready"), sem("wT_done"), sem("wT_copied"), sem("mask_ready"))
        stats_done, mv_done, power_ready, var_ready, rstd_ready = (
            sem("stats_done"), sem("mv_done"), sem("power_ready"), sem("var_ready"), sem("rstd_ready"))
        xr_ready, xr_kept, xrT_kept, xrT_done, xnT_ready, lg_done, lg_ready = (
            sem("xr_ready"), sem("xr_kept"), sem("xrT_kept"), sem("xrT_done"), sem("xnT_ready"), sem("lg_done"), sem("lg_ready"))
        route, counted, gap_ready, gap_exp, pos_ready, wt_ready, eid_ready = (
            sem("route"), sem("counted"), sem("gap_ready"), sem("gap_exp"), sem("pos_ready"), sem("wt_ready"),
            sem("eid_ready"))
        zeroed, scattered = sem("zeroed"), sem("scattered")
        qk_done, prod_done, rot_done, qm_ready, kz_ready, xv_ready = (
            sem("qk_done"), sem("prod_done"), sem("rot_done"), sem("qm_ready"), sem("kz_ready"), sem("xv_ready"))
        v_done, vbd_ready, s_done, max_done, sub_done, exp_done = (
            sem("v_done"), sem("vbd_ready"), sem("s_done"), sem("max_done"), sem("sub_done"), sem("exp_done"))
        sum_done, rc_done, rexp_ready, rT_done, rT_ready = (
            sem("sum_done"), sem("rc_done"), sem("rexp_ready"), sem("rT_done"), sem("rT_ready"))
        t_done, pT_ready, y_done, yT_ready, o_done, acc_done = (
            sem("t_done"), sem("pT_ready"), sem("y_done"), sem("yT_ready"), sem("o_done"), sem("acc_done"))
        xs_in = [sem(f"xs_in{b}") for b in range(2)]
        xsT_done, xsT_ready, wl1_ready, wl2_ready = (
            sem("xsT_done"), sem("xsT_ready"), sem("wl1_ready"), sem("wl2_ready"))
        h_done, hT_ready, yy_done, ys_ready = (
            sem("h_done"), sem("hT_ready"), sem("yy_done"), sem("ys_ready"))
        ys_out = [sem(f"ys_out{b}") for b in range(2)]
        gathered = [sem(f"gathered{b}") for b in range(2)]
        part_done, tile_done, out_done = sem("part_done"), sem("tile_done"), sem("out_done")

        XPART = TILES // 4
        PAIR = 16 * 2 * TOP_K

        def pipeline(eng, step, first, end, lag):
            head = first + lag + 2
            for n in range(first, head):
                step(n, n % 2, lambda s, n=n: n - s >= first)
            with eng.Fori(0, (end - head) // 2, 1) as i:
                for b in range(2):
                    step(i * 2 + (head + b), (head + b) % 2, lambda s: True)
            for n in range(end, end + lag):
                step(n, n % 2, lambda s, n=n: n - s < end)

        def wait_from(eng, semaphore, value):
            if not isinstance(value, int) or value > 0:
                eng.wait_ge(semaphore, value)

        LAG = 4
        HALVES = [(0, HALF), (HALF, TILES)]
        FFN_LAG = 2

        block = ctx.enter_context(nc.Block())

        @block.sync
        def _(sp):
            x_t = x.rearrange("b (t p) c -> p (b t) c", p=P)
            out_t = out.rearrange("b (t p) c -> p (b t) c", p=P)
            for i in range(4):
                sp.dma_start(acc[:, i * XPART:(i + 1) * XPART, :], x_t[:, i * XPART:(i + 1) * XPART, :]).then_inc(x_in[i], 16)
                if i == 0:
                    sp.dma_start(kc[:, :], consts).then_inc(consts_in, 16)
                    sp.dma_start(raw[:, 0:3, :], w_attn.rearrange("(s o) c -> o s c", s=3)).then_inc(wraw_in, 16)
                    sp.dma_start(raw[:, 3, :], w_proj).then_inc(wraw_in, 16)
                    sp.dma_start(raw[0:E * FC, 4, :], b1.rearrange("e (f p) -> (e f) p", p=P)).then_inc(wraw_in, 16)
                    sp.wait_ge(wgate_ready, 1)
                    sp.dma_start(wgate[:, 0:E], gate_w).then_inc(gate_in, 16)
                    sp.dma_start(gbias[:, :], gate_b.rearrange("(a e) -> a e", a=1).partition_broadcast(P)
                                 .rearrange("p a e -> p (a e)")).then_inc(gate_in, 16)
            sp.wait_ge(fills, 1)
            sp.dma_start(xg_dram.rearrange("(t p) c -> p t c", p=P),
                         zeros[:, :].rearrange("p (a c) -> p a c", a=1).to_broadcast([P, SLOT_TILES, C])).then_inc(zeroed, 16)
            sp.dma_start(wall[:, :, 0:F], w1.rearrange("e c f -> c e f")).then_inc(wall_in, 16)
            for e in range(E):
                sp.dma_start(wall[:, e, W_2:W_B2].rearrange("p (k d) -> p k d", k=FC),
                             w2[e].rearrange("(k p) d -> p k d", p=P)).then_inc(wall_in, 16)
            sp.dma_start(wall[:, :, W_B2:W_ALL], b2.rearrange("(a e) d -> a e d", a=1).partition_broadcast(P)
                         .rearrange("p a e d -> p (a e) d")).then_inc(wall_in, 16)

            def load_slots(n, b):
                wait_from(sp, xsT_done, n - 1)
                sp.dma_start(xs[:, b, :], xg_dram[bass.ds(n * P, P), :]).then_inc(xs_in[b], 16)

            sp.wait_ge(scattered, 16 * TOP_K * TILES)
            for n in range(2):
                load_slots(n, n)
            with sp.Fori(0, SLOT_TILES // 2 - 1, 1) as i:
                for b in range(2):
                    load_slots(i * 2 + (b + 2), b)

            with sp.Fori(0, TILES // 2, 1) as i:
                sp.wait_ge(tile_done, i * 2 + 2)
                sp.dma_start(out_t[:, bass.ds(i * 2, 2), :], acc[:, bass.ds(i * 2, 2), :]).then_inc(out_done, 16)
            sp.wait_ge(out_done, 16 * (TILES // 2))

        @block.gpsimd
        def _(pool):
            pool.memset(power[:, :], -0.5).then_inc(power_ready, 1)
            pool.wait_ge(power_ready, 1)
            pool.wait_ge(var_ready, 1)
            pool.tensor_tensor(rstd[:, :], var[:, :], power[:, :], ALU.pow).then_inc(rstd_ready, 1)

            pool.wait_ge(pos_ready, 1)
            pool.wait_ge(zeroed, 16)
            pool.wait_ge(xr_kept, TILES)
            for t in range(TILES):
                for k in range(TOP_K):
                    pool.indirect_dma_start(xg_dram, bass.IndirectOffsetOnAxis(ap=pos[:, k, t:t + 1], axis=0),
                                            xn[:, t, :], None).then_inc(scattered, 16)

            with pool.Fori(0, SLOT_TILES // 2, 1) as i:
                for b in range(2):
                    pool.wait_ge(ys_ready, i * 2 + (b + 1))
                    pool.dma_start(yg_dram[bass.ds((i * 2 + b) * P, P), :], ys[:, b, :]).then_inc(ys_out[b], 16)
            for b in range(2):
                pool.wait_ge(ys_out[b], 8 * SLOT_TILES)

            for t in range(TILES):
                m = t // 2
                if t % 2 == 0 and m >= 2:
                    pool.wait_ge(gathered[m % 2], PAIR * (m // 2))
                for k in range(TOP_K):
                    pool.indirect_dma_start(got[:, k, t, :], None, yg_dram,
                                            bass.IndirectOffsetOnAxis(ap=pos[:, k, t:t + 1], axis=0)).then_inc(gathered[m % 2], 16)

        @block.tensor
        def _(pe):
            ident = kc[:, K_ID:K_ID + P]
            pe.wait_ge(consts_in, 16)
            pe.wait_ge(wraw_in, 48)
            for s in range(4):
                pe.transpose(s_ps[:, 2 * s:2 * s + 2, :], raw[:, s, :], ident)
            pe.transpose(y_ps[:, 0, 0:E * FC], raw[0:E * FC, 4, :], kc[0:E * FC, K_ID:K_ID + E * FC]).then_inc(wT_done, 1)

            pe.wait_ge(gate_in, 32)

            def prelude(n, b, has):
                if has(0):
                    pe.wait_ge(xr_ready, n + 1)
                    wait_from(pe, xnT_ready, n - 1)
                    pe.transpose(t_ps[:, 4 * b, :], xr[:, b, :], ident).then_inc(xrT_done, 1)
                if has(1):
                    pe.wait_ge(xnT_ready, n)
                    wait_from(pe, lg_ready, n - 2)
                    pe.matmul((v_ps if b else m_ps)[:, 0, :], xsT[:, 1 - b, :], wgate[:, :],
                              start=True, stop=True).then_inc(lg_done, 1)

            pipeline(pe, prelude, 0, TILES, 2)

            pe.wait_ge(route, ROUTE_BOTH)
            pe.matmul(y_ps[:, 0:2, :], kc[:, K_TRI:K_TRI + P], both[:, :, :], start=True, stop=True)
            pe.matmul(y_ps[:, 2:4, :], kc[:, K_ONE:K_ONE + P], both[:, :, :], start=True, stop=True).then_inc(counted, 1)

            def attention(n, b, has):
                a = 1 - b
                if has(0):
                    wait_from(pe, prod_done, n)
                    for s in range(4):
                        mm = pe.matmul(qk_ps[:, s, :], wqk[:, s, :], xnT[:, bass.ds(n * P, P)], start=True, stop=True)
                    mm.then_inc(qk_done, 1)
                if has(3):
                    pe.wait_ge(rexp_ready, n - 2)
                    wait_from(pe, rT_ready, n - 3)
                    wait_from(pe, acc_done, n - 4)
                    pe.transpose(m_ps[:, 0, :], rexp[:, :, :, :].rearrange("p g j d -> p (g j d)"), ident).then_inc(rT_done, 1)
                if has(1):
                    pe.wait_ge(qm_ready, n)
                    pe.wait_ge(kz_ready, n)
                    wait_from(pe, sub_done, n - 1)
                    for c in range(2):
                        cs = slice(CHUNK * c, CHUNK * (c + 1))
                        for j in range(NJ):
                            mm = pe.matmul(s_ps[cs, NG * j:NG * (j + 1), :], qm[:, a, j, cs], kz[:, a, :, cs],
                                           start=True, stop=True)
                    mm.then_inc(s_done, 1)
                if has(2):
                    pe.wait_ge(xv_ready, n - 1)
                    wait_from(pe, vbd_ready, n - 2)
                    for c in range(2):
                        mm = pe.matmul(v_ps[:, c, :], xv[:, b, c, :, :].rearrange("p r t -> p (r t)"), wv[:, :],
                                       start=True, stop=True)
                    mm.then_inc(v_done, 1)
                    pe.wait_ge(exp_done, n - 1)
                    wait_from(pe, pT_ready, n - 2)
                    for s in range(8):
                        mm = pe.transpose(t_ps[:, s, :], pr[:, b, 2 * s:2 * s + 2, :].rearrange("p h k -> p (h k)"), ident)
                    mm.then_inc(t_done, 1)
                if has(3):
                    pe.wait_ge(pT_ready, n - 2)
                    pe.wait_ge(vbd_ready, n - 2)
                    wait_from(pe, yT_ready, n - 3)
                    for g in range(2):
                        for c in range(2):
                            for j in range(NJ):
                                mm = pe.matmul(y_ps[CHUNK * g:CHUNK * (g + 1), c, :], vbd[:, a, c, g, 2 * GRP * j:2 * GRP * (j + 1)],
                                               pT[:, a, 2 * j + g, :], start=(j == 0), stop=(j == NJ - 1))
                    mm.then_inc(y_done, 1)
                if has(4):
                    pe.wait_ge(yT_ready, n - 3)
                    pe.wait_ge(rT_ready, n - 2 if has(3) else n - 3)
                    if not has(3):
                        pe.wait_ge(acc_done, n - 4)
                    pe.matmul(m_ps[:, 1, :], yT[:, b, :], wp[:, :], start=True, stop=True).then_inc(o_done, 1)

            def experts(n, b, has):
                a = 1 - b
                if has(0):
                    pe.wait_ge(xs_in[b], (n - b) * 8 + 16)
                    wait_from(pe, xsT_ready, n)
                    pe.transpose(qk_ps[:, 0, :], xs[:, b, :], ident).then_inc(xsT_done, 1)
                if has(1):
                    pe.wait_ge(xsT_ready, n)
                    pe.wait_ge(wl1_ready, n)
                    wait_from(pe, hT_ready, n - 2)
                    for f in range(FC):
                        mm = pe.matmul(s_ps[:, 8 * a + 2 * f:8 * a + 2 * f + 2, :], wl1[:, a, f * P:(f + 1) * P], xsT[:, a, :],
                                       start=True, stop=True)
                    mm.then_inc(h_done, 1)
                if has(2):
                    pe.wait_ge(hT_ready, n - 1)
                    pe.wait_ge(wl2_ready, n - 1)
                    wait_from(pe, ys_ready, n - 2)
                    for f in range(FC):
                        mm = pe.matmul(y_ps[:, 0, :], hT[:, b, f, :], wl2[:, b, f * C:(f + 1) * C],
                                       start=(f == 0), stop=(f == FC - 1))
                    mm.then_inc(yy_done, 1)

            pe.wait_ge(route, ROUTE_END)
            pe.wait_ge(wT_copied, WT_COPIES)
            pe.wait_ge(lg_ready, TILES)
            pipeline(pe, attention, *HALVES[0], LAG)
            pe.wait_ge(sub_done, HALF)
            pe.wait_ge(yT_ready, HALF)
            pe.wait_ge(prod_done, HALF)
            pipeline(pe, experts, 0, SLOT_TILES, FFN_LAG)
            pe.wait_ge(hT_ready, SLOT_TILES)
            pe.wait_ge(ys_ready, SLOT_TILES)
            pe.wait_ge(xsT_ready, SLOT_TILES)
            pipeline(pe, attention, *HALVES[1], LAG)

        @block.scalar
        def _(act):
            act.wait_ge(wT_done, 1)
            act.copy(wall[:, :, W_B1:W_2], y_ps[:, 0, 0:E * FC].rearrange("p (e f) -> p e f", e=E)).then_inc(wT_copied, 1)
            for s, to in enumerate((wqk[:, 0, :], wqk[:, 1, :], wv[:, :], wp[:, :])):
                act.copy(to.rearrange("p (a c) -> p a c", a=2), s_ps[:, 2 * s:2 * s + 2, :]).then_inc(wT_copied, 1)
            for s in range(2):
                src = s_ps[:, 2 * s:2 * s + 2, :].rearrange("p a (h u d) -> p (a h) u d", u=2, d=HD // 2)
                dst = wqk[:, 2 + s, :].rearrange("p (h u d) -> p h u d", u=2, d=HD // 2)
                for u in range(2):
                    act.copy(dst[:, :, u, :], src[:, :, 1 - u, :]).then_inc(wT_copied, 1)

            def prelude(n, b, has):
                if has(0):
                    act.wait_ge(xr_ready, n + 1)
                    act.copy(xn[:, bass.ds(n, 1), :], xr[:, b:b + 1, :]).then_inc(xr_kept, 1)
                if has(0):
                    act.wait_ge(xrT_done, n + 1)
                    act.copy(xnT[:, bass.ds(n * P, P)], t_ps[:, 4 * b, :]).then_inc(xrT_kept, 1)
                    wait_from(act, lg_done, n - 1)
                    act.copy(xsT[:, b, :], t_ps[:, 4 * b, :]).then_inc(xnT_ready, 1)

            pipeline(act, prelude, 0, TILES, 2)

            act.wait_ge(gap_ready, 1)
            act.activation(den[:, :], gap[:, :], ACT.Exp).then_inc(gap_exp, 1)

            def attention(n, b, has):
                a = 1 - b
                if has(3):
                    act.wait_ge(rT_done, n - 2)
                    wait_from(act, yT_ready, n - 3)
                    act.copy(rT[:, :], m_ps[:, 0, :]).then_inc(rT_ready, 1)
                if has(0):
                    act.wait_ge(rot_done, n + 1)
                    wait_from(act, s_done, n - 1)
                    for g in range(NG):
                        gs = slice(32 * g, 32 * (g + 1))
                        ins = act.copy(kz[gs, b, g, :], rot[gs, 1, :])
                    ins.then_inc(kz_ready, 1)
                if has(1):
                    wait_from(act, v_done, n - 2)
                    act.copy(xv[:, a, :, :, :],
                             xnT[:, bass.ds((n - 1) * P, P)].rearrange("p (c r t) -> p c r t", c=2, r=1)
                             .to_broadcast([P, 2, 2, CHUNK])).then_inc(xv_ready, 1)
                if has(2):
                    act.wait_ge(v_done, n - 1)
                    wait_from(act, y_done, n - 3)
                    for c in range(2):
                        for r in range(2):
                            rs = slice(CHUNK * r, CHUNK * (r + 1))
                            src = v_ps[rs, c, :].rearrange("p (g r j d) -> p j g r d", g=2, r=2, j=NJ)[:, :, :, r, :]
                            dst = vbd[rs, b, c, :, :].rearrange("p g (j w) -> p j g w", j=NJ)[:, :, :, GRP * r:GRP * r + HD]
                            ins = act.copy(dst, src)
                    ins.then_inc(vbd_ready, 1)
                    act.wait_ge(t_done, n - 1)
                    wait_from(act, y_done, n - 3)
                    act.copy(pT[:, b, :, :], t_ps[:, :, :]).then_inc(pT_ready, 1)
                if has(1):
                    act.wait_ge(sub_done, n)
                    act.activation(pr[:, a, :, :], pr[:, a, :, :], ACT.Exp, scale=SCALE).then_inc(exp_done, 1)

            def experts(n, b, has):
                a = 1 - b
                if has(1):
                    act.wait_ge(h_done, n)
                    wait_from(act, yy_done, n - 2)
                    for f in range(FC):
                        ins = act.activation(hT[:, a, f, :], s_ps[:, 8 * a + 2 * f:8 * a + 2 * f + 2, :].rearrange("p a c -> p (a c)"),
                                             ACT.Gelu, bias=wl1[:, a, F + f:F + f + 1])
                    ins.then_inc(hT_ready, 1)

            act.wait_ge(fills, 3)
            act.wait_ge(xrT_kept, TILES)
            pipeline(act, attention, *HALVES[0], LAG)
            pipeline(act, experts, 0, SLOT_TILES, FFN_LAG)
            pipeline(act, attention, *HALVES[1], LAG)

        @block.vector
        def _(dve):
            dve.memset(wgate[:, :], 0.0).then_inc(wgate_ready, 1)
            dve.memset(zeros[:, :], 0.0).then_inc(fills, 1)
            dve.memset(kz[:, :, :, :], 0.0).then_inc(fills, 1)
            dve.memset(vbd[:, :, :, :, :], 0.0).then_inc(fills, 1)

            for i in range(4):
                dve.wait_ge(x_in[i], 16)
                for t in range(i * XPART, (i + 1) * XPART):
                    dve.bn_stats(stats[:, t, :], acc[:, t, :]).then_inc(stats_done, 1)
                for t in range(i * XPART, (i + 1) * XPART):
                    dve.wait_ge(stats_done, t + 1)
                    dve.bn_aggr(mv[:, t, :], stats[:, t, :]).then_inc(mv_done, 1)
            dve.wait_ge(mv_done, TILES)
            dve.tensor_scalar(var[:, :], mv[:, :, 1], EPS, None, ALU.add).then_inc(var_ready, 1)
            dve.wait_ge(consts_in, 16)
            for j in range(NJ):
                dve.tensor_copy(mask[:, j, :], kc[:, K_MASK + j:K_MASK + j + 1].to_broadcast([P, P])).then_inc(mask_ready, 1)
            dve.wait_ge(rstd_ready, 1)
            dve.wait_ge(gate_in, 32)

            def prelude(n, b, has):
                if has(0):
                    wait_from(dve, xrT_done, n - 1)
                    wait_from(dve, xr_kept, n - 1)
                    dve.tensor_scalar(xr[:, b:b + 1, :], acc[:, bass.ds(n, 1), :], mv[:, bass.ds(n, 1), 0:1].rearrange("p a b -> p (a b)"),
                                      rstd[:, bass.ds(n, 1)], ALU.subtract, ALU.mult).then_inc(xr_ready, 1)
                if has(2):
                    dve.wait_ge(lg_done, n - 1)
                    dve.tensor_tensor(lg[:, bass.ds(n - 2, 1), :], (m_ps if b else v_ps)[:, 0:1, 0:E],
                                      gbias[:, :].rearrange("p (a e) -> p a e", a=1), ALU.add).then_inc(lg_ready, 1)

            pipeline(dve, prelude, 0, TILES, 2)

            steps = [0]

            def then_route(ins):
                ins.then_inc(route, 1)
                steps[0] += 1
                dve.wait_ge(route, steps[0])

            def over_e(v):
                return v.rearrange("p (t a) -> p t a", a=1).to_broadcast([P, TILES, E])

            e8 = kc[:, K_E8:K_E8 + E].rearrange("p (a e) -> p a e", a=1).to_broadcast([P, TILES, E])
            dve.wait_ge(lg_ready, TILES)
            for k in range(2):
                then_route(dve.tensor_reduce(best[:, k, :], lg[:, :, :], AX.X, ALU.max))
                then_route(dve.tensor_tensor(work[:, :, :], lg[:, :, :], over_e(best[:, k, :]), ALU.is_equal))
                then_route(dve.tensor_tensor(work[:, :, :], work[:, :, :], e8, ALU.mult))
                then_route(dve.tensor_reduce(pick[:, k, :], work[:, :, :], AX.X, ALU.min))
                then_route(dve.tensor_tensor(hot[:, k, :, :], e8, over_e(pick[:, k, :]), ALU.is_equal))
                if k == 0:
                    then_route(dve.scalar_tensor_tensor(out=lg[:, :, :], in0=hot[:, 0, :, :], scalar=FAR, in1=lg[:, :, :],
                                                        op0=ALU.mult, op1=ALU.add))
            then_route(dve.tensor_tensor(both[:, :, :].rearrange("p e t -> p t e"), hot[:, 0, :, :], hot[:, 1, :, :], ALU.add))
            assert steps[0] == ROUTE_BOTH
            dve.tensor_tensor(gap[:, :], best[:, 1, :], best[:, 0, :], ALU.subtract).then_inc(gap_ready, 1)
            dve.wait_ge(counted, 1)
            total = y_ps[:, 2:4, :].rearrange("p a c -> p (a c)")
            then_route(dve.tensor_copy(place[:, :, :].rearrange("p e t -> p (e t)"), total))
            then_route(dve.tensor_tensor_scan(run[:, :], kc[:, K_ONE:K_ONE + 1].to_broadcast([P, E * TILES]),
                                              place[:, :, :].rearrange("p e t -> p (e t)"), 0.0, ALU.mult, ALU.add))
            run_e = run[:, :].rearrange("p (e t) -> p e t", e=E)
            then_route(dve.tensor_tensor(place[:, :, :], run_e, place[:, :, :], ALU.subtract))
            then_route(dve.tensor_tensor(place[:, :, :].rearrange("p e t -> p (e t)"), place[:, :, :].rearrange("p e t -> p (e t)"),
                                         y_ps[:, 0:2, :].rearrange("p a c -> p (a c)"), ALU.add))
            then_route(dve.tensor_copy(load_e[:, 0:1], run_e[:, 0, TILES - 1:TILES]))
            then_route(dve.tensor_tensor(load_e[:, 1:E], run_e[:, 1:E, TILES - 1], run_e[:, 0:E - 1, TILES - 1], ALU.subtract))
            then_route(dve.tensor_tensor(many[:, :, :], load_e[:, :].rearrange("p (e a) -> p e a", a=1).to_broadcast([P, E, TILES]),
                                         kc[:, K_STEP:K_STEP + TILES].rearrange("p (a t) -> p a t", a=1).to_broadcast([P, E, TILES]),
                                         ALU.is_gt))
            then_route(dve.tensor_reduce(padded[:, :], many[:, :, :], AX.X, ALU.add))
            then_route(dve.tensor_scalar(padded[:, :], padded[:, :], float(P), None, ALU.mult))
            then_route(dve.tensor_tensor_scan(ends[:, :], kc[:, K_ONE:K_ONE + 1].to_broadcast([P, E]), padded[:, :], 0.0,
                                              ALU.mult, ALU.add))
            then_route(dve.tensor_tensor(shift[:, :], ends[:, :], padded[:, :], ALU.subtract))
            then_route(dve.tensor_tensor(shift[:, :], shift[:, :], run_e[:, :, TILES - 1], ALU.subtract))
            then_route(dve.tensor_tensor(shift[:, :], shift[:, :], load_e[:, :], ALU.add))
            then_route(dve.tensor_tensor(place[:, :, :], place[:, :, :],
                                         shift[:, :].rearrange("p (e a) -> p e a", a=1).to_broadcast([P, E, TILES]), ALU.add))
            for k in range(2):
                then_route(dve.tensor_tensor(work[:, :, :], hot[:, k, :, :], place[:, :, :].rearrange("p e t -> p t e"), ALU.mult))
                then_route(dve.tensor_reduce(posf[:, k, :], work[:, :, :], AX.X, ALU.add))
            dve.tensor_copy(pos[:, :, :], posf[:, :, :]).then_inc(pos_ready, 1)
            then_route(dve.tensor_tensor(late[:, :, :],
                                         kc[0:1, K_START:K_START + SLOT_TILES].rearrange("p (t a) -> p t a", a=1).to_broadcast([1, SLOT_TILES, E]),
                                         ends[0:1, :].rearrange("p (a e) -> p a e", a=1).to_broadcast([1, SLOT_TILES, E]), ALU.is_ge))
            then_route(dve.tensor_reduce(eidf[:, :], late[:, :, :], AX.X, ALU.add))
            then_route(dve.tensor_scalar(eidf[:, :], eidf[:, :], float(E - 1), None, ALU.min))
            dve.tensor_copy(eid[:, :], eidf[:, :]).then_inc(eid_ready, 1)
            dve.wait_ge(gap_exp, 1)
            then_route(dve.tensor_scalar(wt[:, 1, :], den[:, :], 1.0, None, ALU.add))
            then_route(dve.reciprocal(wt[:, 0, :], wt[:, 1, :]))
            assert steps[0] == ROUTE_END - 1
            then_route(dve.tensor_tensor(wt[:, 1, :], den[:, :], wt[:, 0, :], ALU.mult))

            cos = kc[:, K_COS:K_COS + CHUNK].rearrange("p (a b t) -> p a b t", a=1, b=1).to_broadcast([P, 2, 2, CHUNK])
            sin = kc[:, K_SIN:K_SIN + CHUNK].rearrange("p (a b t) -> p a b t", a=1, b=1).to_broadcast([P, 2, 2, CHUNK])

            def attention(n, b, has):
                a = 1 - b
                if has(2):
                    dve.wait_ge(exp_done, n - 1)
                    wait_from(dve, rc_done, n - 2)
                    dve.tensor_reduce(sm[:, :], pr[:, b, :, :], AX.X, ALU.add).then_inc(sum_done, 1)
                    dve.wait_ge(sum_done, n - 1)
                    wait_from(dve, rexp_ready, n - 2)
                    dve.reciprocal(rc[:, :], sm[:, :]).then_inc(rc_done, 1)
                    dve.wait_ge(rc_done, n - 1)
                    wait_from(dve, rT_done, n - 2)
                    dve.tensor_copy(rexp[:, :, :, :].rearrange("p g j d -> p j g d"),
                                    rc[:, :].rearrange("p (j g a) -> p j g a", j=NJ, a=1).to_broadcast([P, NJ, NG, HD])
                                    ).then_inc(rexp_ready, 1)
                if has(0):
                    dve.wait_ge(qk_done, n + 1)
                    wait_from(dve, rot_done, n)
                    dve.tensor_tensor(rp[:, 0:2, :].rearrange("p s (c t) -> p s c t", c=2),
                                      qk_ps[:, 0:2, :].rearrange("p s (c t) -> p s c t", c=2), cos, ALU.mult)
                    dve.tensor_tensor(rp[:, 2:4, :].rearrange("p s (c t) -> p s c t", c=2),
                                      qk_ps[:, 2:4, :].rearrange("p s (c t) -> p s c t", c=2), sin, ALU.mult).then_inc(prod_done, 1)
                    dve.wait_ge(prod_done, n + 1)
                    wait_from(dve, kz_ready, n)
                    wait_from(dve, qm_ready, n)
                    dve.tensor_tensor(rot[:, :, :], rp[:, 0:2, :], rp[:, 2:4, :], ALU.add).then_inc(rot_done, 1)
                    dve.wait_ge(rot_done, n + 1)
                    wait_from(dve, s_done, n - 1)
                    dve.tensor_tensor(qm[:, b, :, :], rot[:, 0:1, :].to_broadcast([P, NJ, P]), mask[:, :, :], ALU.mult).then_inc(qm_ready, 1)
                if has(1):
                    dve.wait_ge(s_done, n)
                    wait_from(dve, sub_done, n - 1)
                    dve.tensor_reduce(mx[:, :], s_ps[:, :, :], AX.X, ALU.max).then_inc(max_done, 1)
                    dve.wait_ge(max_done, n)
                    wait_from(dve, t_done, n - 2)
                    wait_from(dve, sum_done, n - 2)
                    dve.tensor_tensor(pr[:, a, :, :], s_ps[:, :, :],
                                      mx[:, :].rearrange("p (h a) -> p h a", a=1).to_broadcast([P, NJ * NG, CHUNK]),
                                      ALU.subtract).then_inc(sub_done, 1)
                if has(3):
                    dve.wait_ge(y_done, n - 2)
                    dve.wait_ge(rT_ready, n - 2)
                    wait_from(dve, o_done, n - 4)
                    for c in range(2):
                        cs = slice(CHUNK * c, CHUNK * (c + 1))
                        ins = dve.tensor_tensor(yT[:, a, cs], y_ps[:, c, cs], rT[:, cs], ALU.mult)
                    ins.then_inc(yT_ready, 1)
                if has(4):
                    dve.wait_ge(o_done, n - 3)
                    dve.tensor_tensor(acc[:, bass.ds(n - 4, 1), :], acc[:, bass.ds(n - 4, 1), :], m_ps[:, 1:2, :],
                                      ALU.add).then_inc(acc_done, 1)

            def combine(m, b, t0):
                dve.wait_ge(gathered[b], (m - b) * (PAIR // 2) + PAIR)
                for k in range(TOP_K):
                    for u in range(2):
                        here = acc[:, bass.ds(t0 + u, 1), :]
                        ins = dve.scalar_tensor_tensor(out=here, in0=got[:, k, bass.ds(t0 + u, 1), :],
                                                       scalar=wt[:, k, bass.ds(t0 + u, 1)], in1=here,
                                                       op0=ALU.mult, op1=ALU.add)
                        ins.then_inc(part_done if k == 0 else tile_done, 1)
                    if k == 0:
                        dve.wait_ge(part_done, (m + 1) * 2)

            def attention_and_combine(n, b, has):
                attention(n, b, has)
                if has(4):
                    dve.wait_ge(acc_done, n - 3)
                    combine(n - (4 + HALF), b, (n - (4 + HALF)) * 2)

            def expert_of(n):
                return nc.vector.value_load(eid[0:1, bass.ds(n, 1)], min_val=0, max_val=E - 1)

            def experts(n, b, has):
                a = 1 - b
                if has(0):
                    e = expert_of(n)
                    dve.wait_ge(xsT_done, n + 1)
                    wait_from(dve, h_done, n - 1)
                    dve.tensor_copy(xsT[:, b, :], qk_ps[:, 0, :]).then_inc(xsT_ready, 1)
                    wait_from(dve, hT_ready, n - 1)
                    dve.tensor_copy(wl1[:, b:b + 1, :], wall[:, bass.ds(e, 1), 0:W_2]).then_inc(wl1_ready, 1)
                if has(1):
                    e = expert_of(n - 1)
                    wait_from(dve, yy_done, n - 2)
                    wait_from(dve, ys_ready, n - 2)
                    dve.tensor_copy(wl2[:, a:a + 1, :], wall[:, bass.ds(e, 1), W_2:W_ALL]).then_inc(wl2_ready, 1)
                if has(2):
                    dve.wait_ge(yy_done, n - 1)
                    wait_from(dve, ys_out[b], (n - (2 + b)) * 8)
                    dve.tensor_tensor(ys[:, b, :], y_ps[:, 0, :], wl2[:, b, FC * C:FC * C + C], ALU.add).then_inc(ys_ready, 1)

            pipeline(dve, attention, *HALVES[0], LAG)
            dve.wait_ge(wall_in, 16 * (E + 2))
            dve.wait_ge(wT_copied, 1)
            dve.wait_ge(eid_ready, 1)
            pipeline(dve, experts, 0, SLOT_TILES, FFN_LAG)
            pipeline(dve, attention_and_combine, *HALVES[1], LAG)


ROUTE_BOTH = 12
ROUTE_END = ROUTE_BOTH + 14 + 4 + 3 + 3
WT_COPIES = 9

_INS = ["L0_attn_x", "L0_attn_w_attn", "L0_attn_w_proj", "L0_ffn_gate_w", "L0_ffn_gate_b",
        "L0_ffn_w1", "L0_ffn_b1", "L0_ffn_w2", "L0_ffn_b2"]


def kernel(**inputs):
    import concourse.bacc as bacc
    from concourse.bass_utils import run_bass_kernel_spmd

    nc = bacc.Bacc("TRN2", target_bir_lowering=False, num_devices=1)
    arrays = {"in_" + n: np.ascontiguousarray(inputs[n]) for n in _INS}
    arrays["in_consts"] = constants()
    aps = [nc.dram_tensor(n, a.shape, mybir.dt.from_np(a.dtype), kind="ExternalInput").ap() for n, a in arrays.items()]
    out = nc.dram_tensor("out_0", (BATCH, SEQ, C), F32, kind="ExternalOutput").ap()
    build(nc, *aps, out)
    r = run_bass_kernel_spmd(nc, [arrays], core_ids=[0])
    return r.results[0]["out_0"]
```

```python
from contextlib import ExitStack

import numpy as np

import concourse.bass as bass
from concourse import mybir

F32 = mybir.dt.float32
I32 = mybir.dt.int32
ALU = mybir.AluOpType
ACT = mybir.ActivationFunctionType
AX = mybir.AxisListType

P = 128
BATCH, SEQ, C = 2, 2048, 128
TOKENS = BATCH * SEQ
TILES = TOKENS // P
HALF = TILES // 2
HEADS, CHUNK = 16, 64
HD = C // HEADS
NJ, NG = 4, 4
GRP = NJ * HD
DIAG = 2 * GRP + HD
SCALE = 1.0 / float(np.sqrt(HD))
ROPE_BASE = 10000.0
EPS = 1e-5
E, F, TOP_K = 8, 512, 2
FC = F // P
SLOT_TILES = TOKENS * TOP_K // P + E
SLOTS = SLOT_TILES * P
FAR = -3.0e38

K_ID, K_COS, K_SIN, K_MASK = 0, P, P + CHUNK, P + 2 * CHUNK
K_TRI = K_MASK + NJ
K_ONE = K_TRI + P
K_E8 = K_ONE + P
K_STEP = K_E8 + E
K_START = K_STEP + TILES
K_ALL = K_START + SLOT_TILES

W_B1, W_2, W_B2 = F, F + FC, F + FC + FC * C
W_ALL = W_B2 + C


def constants():
    k = np.zeros((P, K_ALL), np.float32)
    k[:, K_ID:K_ID + P] = np.eye(P)
    row = np.arange(P)
    d = row % HD
    freq = (np.float32(1.0) / np.float32(ROPE_BASE) ** (np.arange(0, HD, 2, dtype=np.float32) / np.float32(HD))).astype(np.float32)
    angle = np.outer(freq[d % (HD // 2)], np.arange(CHUNK, dtype=np.float32)).astype(np.float32)
    k[:, K_COS:K_COS + CHUNK] = np.cos(angle)
    k[:, K_SIN:K_SIN + CHUNK] = np.sin(angle) * np.where(d < HD // 2, 1.0, -1.0)[:, None]
    for j in range(NJ):
        k[:, K_MASK + j] = (row // HD) % NJ == j
    k[:, K_TRI:K_TRI + P] = row[:, None] < row[None, :]
    k[:, K_ONE:K_ONE + P] = 1.0
    k[:, K_E8:K_E8 + E] = np.arange(E) - E
    k[:, K_STEP:K_STEP + TILES] = np.arange(TILES) * P
    k[:, K_START:K_START + SLOT_TILES] = np.arange(SLOT_TILES) * P
    return k


def build(nc, x, w_attn, w_proj, gate_w, gate_b, w1, b1, w2, b2, consts, out):
    with ExitStack() as ctx:
        def sb(name, shape, dt=F32):
            return ctx.enter_context(nc.sbuf_tensor("sb_" + name, shape, dt))

        def sem(name):
            return ctx.enter_context(nc.semaphore(name))

        xg_dram = nc.dram_tensor("slot_rows", [SLOTS, C], F32).ap()
        yg_dram = nc.dram_tensor("slot_results", [SLOTS, C], F32).ap()

        kc = sb("consts", [P, K_ALL])
        acc = sb("acc", [P, TILES, C])
        xn = sb("xn", [P, TILES, C])
        xnT = sb("xnT", [P, TOKENS])
        wall = sb("expert_weights", [P, E, W_ALL])
        wqk = sb("wqk", [P, 4, P])
        wv = sb("wv", [P, P])
        wp = sb("wp", [P, P])
        raw = sb("raw_weights", [P, 5, P])
        wgate = sb("wgate", [P, P])
        gbias = sb("gbias", [P, E])
        zeros = sb("zeros", [P, P])
        table = sb("rope_table", [P, 4, P])

        stats = sb("stats", [P, TILES, 6])
        mv = sb("mv", [P, TILES, 2])
        var = sb("var", [P, TILES])
        power = sb("power", [P, TILES])
        rstd = sb("rstd", [P, TILES])

        lg = sb("logits", [P, TILES, E])
        best = sb("best", [P, 2, TILES])
        pick = sb("pick", [P, 2, TILES])
        work = sb("work", [P, TILES, E])
        hot = sb("hot", [P, 2, TILES, E])
        both = sb("both", [P, E, TILES])
        run = sb("run", [P, E * TILES])
        place = sb("place", [P, E, TILES])
        load_e = sb("load_e", [P, E])
        many = sb("many", [P, E, TILES])
        padded = sb("padded", [P, E])
        ends = sb("ends", [P, E])
        shift = sb("shift", [P, E])
        posf = sb("posf", [P, 2, TILES])
        pos = sb("pos", [P, 2, TILES], I32)
        late = sb("late", [1, SLOT_TILES, E])
        eidf = sb("eidf", [1, SLOT_TILES])
        eid = sb("eid", [1, SLOT_TILES], I32)
        gap = sb("gap", [P, TILES])
        den = sb("den", [P, TILES])
        wt = sb("wt", [P, 2, TILES])

        rp = sb("rope_products", [P, 4, P])
        rot = sb("rot", [P, 2, P])
        qm = sb("qm", [P, 2, NJ, P])
        kz = sb("kz", [P, 2, NG, P])
        xv = sb("xv", [P, 2, 2, 2, CHUNK])
        vbd = sb("vbd", [P, 2, 2, 2, NJ * DIAG])
        pr = sb("probs", [P, 2, NJ * NG, CHUNK])
        pT = sb("probsT", [P, 2, NJ * 2, P])
        mx = sb("mx", [P, NJ * NG])
        sm = sb("sm", [P, NJ * NG])
        rc = sb("rc", [P, NJ * NG])
        rexp = sb("rexp", [P, NG, NJ, HD])
        rT = sb("rT", [P, P])
        yT = sb("yT", [P, 2, P])

        xs = sb("xs", [P, 4, P])
        xsT = sb("xsT", [P, 2, P])
        wl1 = sb("wl1", [P, 2, W_2])
        wl2 = sb("wl2", [P, 2, W_ALL - W_2])
        hT = sb("hT", [P, 2, FC, P])
        ys = sb("ys", [P, 4, P])
        got = sb("got", [P, 2, TILES, C])

        qk_ps = ctx.enter_context(nc.psum_tensor("qk_ps", [P, 4, P], F32))
        v_ps = ctx.enter_context(nc.psum_tensor("v_ps", [P, 4, P], F32))
        s_ps = ctx.enter_context(nc.psum_tensor("s_ps", [P, NJ * NG, CHUNK], F32))
        t_ps = ctx.enter_context(nc.psum_tensor("t_ps", [P, 8, P], F32))
        y_ps = ctx.enter_context(nc.psum_tensor("y_ps", [P, 4, P], F32))
        m_ps = ctx.enter_context(nc.psum_tensor("m_ps", [P, 4, P], F32))

        x_in = [sem(f"x_in{i}") for i in range(4)]
        consts_in, wraw_in, gate_in, wall_in = sem("consts_in"), sem("wraw_in"), sem("gate_in"), sem("wall_in")
        fills, wgate_ready, wT_done, wT_copied, table_ready = (
            sem("fills"), sem("wgate_ready"), sem("wT_done"), sem("wT_copied"), sem("table_ready"))
        stats_done, mv_done, power_ready, var_ready, rstd_ready = (
            sem("stats_done"), sem("mv_done"), sem("power_ready"), sem("var_ready"), sem("rstd_ready"))
        xn_ready, xnT_done, xnT_ready, lg_done, lg_ready = (
            sem("xn_ready"), sem("xnT_done"), sem("xnT_ready"), sem("lg_done"), sem("lg_ready"))
        route, counted, gap_ready, gap_exp, pos_ready, wt_ready, eid_ready = (
            sem("route"), sem("counted"), sem("gap_ready"), sem("gap_exp"), sem("pos_ready"), sem("wt_ready"),
            sem("eid_ready"))
        zeroed, scattered = sem("zeroed"), sem("scattered")
        qk_done, prod_done, rot_done, qm_ready, kz_ready, xv_ready = (
            sem("qk_done"), sem("prod_done"), sem("rot_done"), sem("qm_ready"), sem("kz_ready"), sem("xv_ready"))
        v_done, vbd_ready, s_done, max_done, sub_done, exp_done = (
            sem("v_done"), sem("vbd_ready"), sem("s_done"), sem("max_done"), sem("sub_done"), sem("exp_done"))
        sum_done, rc_done, rexp_ready, rT_done, rT_ready = (
            sem("sum_done"), sem("rc_done"), sem("rexp_ready"), sem("rT_done"), sem("rT_ready"))
        t_done, pT_ready, y_done, yT_ready, o_done, acc_done = (
            sem("t_done"), sem("pT_ready"), sem("y_done"), sem("yT_ready"), sem("o_done"), sem("acc_done"))
        xs_in = [sem(f"xs_in{b}") for b in range(2)]
        xsT_done, xsT_ready, wl1_ready, wl2_ready = (
            sem("xsT_done"), sem("xsT_ready"), sem("wl1_ready"), sem("wl2_ready"))
        h_done, hT_ready, yy_done, ys_ready = (
            sem("h_done"), sem("hT_ready"), sem("yy_done"), sem("ys_ready"))
        ys_out = [sem(f"ys_out{b}") for b in range(2)]
        gathered = [sem(f"gathered{b}") for b in range(2)]
        part_done, tile_done, out_done = sem("part_done"), sem("tile_done"), sem("out_done")

        XPART = TILES // 4
        PAIR = 16 * 2 * TOP_K

        def at(n, k):
            return isinstance(n, int) and n == k

        def steady(eng, step, first, end, unroll):
            assert (end - first) % unroll == 0
            with eng.Fori(0, (end - first) // unroll, 1) as i:
                for b in range(unroll):
                    step(i * unroll + (first + b), (first + b) % RING, lambda s: True)

        def tail(step, end, first, count):
            for n in range(first, first + count):
                step(n, n % RING, lambda s, n=n: n - s < end)

        def everything(eng, attention, experts, second_attention, between):
            for k in range(HEAD):
                attention(k, k % RING, lambda s: k - s >= 0)
                between(k)
            steady(eng, attention, HEAD, HALF, 2)
            for k in range(LAG):
                tail(attention, HALF, HALF + k, 1)
                experts(k, k % RING, lambda s: k - s >= 0)
            for k in range(LAG, EXPERTS_HEAD):
                experts(k, k % RING, lambda s: True)
            steady(eng, experts, EXPERTS_HEAD, SLOT_TILES, RING)
            for k in range(EXPERTS_LAG):
                tail(experts, SLOT_TILES, SLOT_TILES + k, 1)
                second_attention(HALF + k, (HALF + k) % RING, lambda s: k - s >= 0)
            for k in range(EXPERTS_LAG, HEAD):
                second_attention(HALF + k, (HALF + k) % RING, lambda s: k - s >= 0)
            steady(eng, second_attention, HALF + HEAD, TILES, 2)
            tail(second_attention, TILES, TILES, LAG)

        def wait_from(eng, semaphore, value):
            if not isinstance(value, int) or value > 0:
                eng.wait_ge(semaphore, value)

        RING = 4
        LAG, EXPERTS_LAG = 4, 2
        HEAD, EXPERTS_HEAD = 6, 8

        block = ctx.enter_context(nc.Block())

        @block.sync
        def _(sp):
            x_t = x.rearrange("b (t p) c -> p (b t) c", p=P)
            out_t = out.rearrange("b (t p) c -> p (b t) c", p=P)
            for i in range(4):
                sp.dma_start(acc[:, i * XPART:(i + 1) * XPART, :], x_t[:, i * XPART:(i + 1) * XPART, :]).then_inc(x_in[i], 16)
                if i == 0:
                    sp.dma_start(kc[:, :], consts).then_inc(consts_in, 16)
            sp.wait_ge(wgate_ready, 1)
            sp.dma_start(wgate[:, 0:E], gate_w).then_inc(gate_in, 16)
            sp.dma_start(gbias[:, :], gate_b.rearrange("(a e) -> a e", a=1).partition_broadcast(P)
                         .rearrange("p a e -> p (a e)")).then_inc(gate_in, 16)
            sp.dma_start(raw[:, 0:3, :], w_attn.rearrange("(s o) c -> o s c", s=3)).then_inc(wraw_in, 16)
            sp.dma_start(raw[:, 3, :], w_proj).then_inc(wraw_in, 16)
            sp.dma_start(raw[0:E * FC, 4, :], b1.rearrange("e (f p) -> (e f) p", p=P)).then_inc(wraw_in, 16)
            sp.wait_ge(fills, 1)
            sp.dma_start(xg_dram.rearrange("(t p) c -> p t c", p=P),
                         zeros[:, :].rearrange("p (a c) -> p a c", a=1).to_broadcast([P, SLOT_TILES, C])).then_inc(zeroed, 16)
            sp.dma_start(wall[:, :, 0:F], w1.rearrange("e c f -> c e f")).then_inc(wall_in, 16)
            for e in range(E):
                sp.dma_start(wall[:, e, W_2:W_B2].rearrange("p (k d) -> p k d", k=FC),
                             w2[e].rearrange("(k p) d -> p k d", p=P)).then_inc(wall_in, 16)
            sp.dma_start(wall[:, :, W_B2:W_ALL], b2.rearrange("(a e) d -> a e d", a=1).partition_broadcast(P)
                         .rearrange("p a e d -> p (a e) d")).then_inc(wall_in, 16)

            xg_t = xg_dram.rearrange("(t p) c -> p t c", p=P)
            yg_t = yg_dram.rearrange("(t p) c -> p t c", p=P)

            def load_slots(m, b):
                sp.dma_start(xs[:, 2 * b:2 * b + 2, :], xg_t[:, bass.ds(m * 2, 2), :]).then_inc(xs_in[b], 16)

            def store_slots(m, b):
                sp.wait_ge(ys_ready, m * 2 + 2)
                sp.dma_start(yg_t[:, bass.ds(m * 2, 2), :], ys[:, 2 * b:2 * b + 2, :]).then_inc(ys_out[b], 16)

            sp.wait_ge(scattered, 16 * TOP_K * TILES)
            for m in range(2):
                load_slots(m, m)
            with sp.Fori(0, SLOT_TILES // 4 - 1, 1) as i:
                for b in range(2):
                    sp.wait_ge(xsT_done, i * 4 + (2 * b + 2))
                    load_slots(i * 2 + (b + 2), b)
                    store_slots(i * 2 + b, b)
            for m in range(SLOT_TILES // 2 - 2, SLOT_TILES // 2):
                store_slots(m, m % 2)

            with sp.Fori(0, TILES // 2, 1) as i:
                sp.wait_ge(tile_done, i * 2 + 2)
                sp.dma_start(out_t[:, bass.ds(i * 2, 2), :], acc[:, bass.ds(i * 2, 2), :]).then_inc(out_done, 16)
            sp.wait_ge(out_done, 16 * (TILES // 2))

        @block.gpsimd
        def _(pool):
            pool.memset(power[:, :], -0.5).then_inc(power_ready, 1)
            pool.wait_ge(power_ready, 1)
            for i in range(4):
                ts = slice(i * XPART, (i + 1) * XPART)
                pool.wait_ge(var_ready, i + 1)
                pool.tensor_tensor(rstd[:, ts], var[:, ts], power[:, ts], ALU.pow).then_inc(rstd_ready, 1)

            pool.wait_ge(pos_ready, 1)
            pool.wait_ge(zeroed, 16)
            pool.wait_ge(xn_ready, 4)
            for t in range(TILES):
                for k in range(TOP_K):
                    pool.indirect_dma_start(xg_dram, bass.IndirectOffsetOnAxis(ap=pos[:, k, t:t + 1], axis=0),
                                            xn[:, t, :], None).then_inc(scattered, 16)

            for b in range(2):
                pool.wait_ge(ys_out[b], 16 * (SLOT_TILES // 4))

            for t in range(TILES):
                m = t // 2
                if t % 2 == 0 and m >= 2:
                    pool.wait_ge(gathered[m % 2], PAIR * (m // 2))
                for k in range(TOP_K):
                    pool.indirect_dma_start(got[:, k, t, :], None, yg_dram,
                                            bass.IndirectOffsetOnAxis(ap=pos[:, k, t:t + 1], axis=0)).then_inc(gathered[m % 2], 16)

        @block.tensor
        def _(pe):
            ident = kc[:, K_ID:K_ID + P]
            pe.wait_ge(consts_in, 16)
            pe.wait_ge(gate_in, 32)

            for g in range(TILES // 4 + 1):
                if g < TILES // 4:
                    pe.wait_ge(xn_ready, g // 2 + 1)
                    wait_from(pe, xnT_ready, g - 1)
                    for u in range(4):
                        mm = pe.transpose(t_ps[:, 4 * (g % 2) + u, :], xn[:, 4 * g + u, :], ident)
                    mm.then_inc(xnT_done, 1)
                if g >= 1:
                    pe.wait_ge(xnT_ready, g)
                    wait_from(pe, lg_ready, g - 2)
                    for u in range(4):
                        t = 4 * (g - 1) + u
                        mm = pe.matmul((v_ps if g % 2 else m_ps)[:, u, :], xnT[:, t * P:(t + 1) * P], wgate[:, :],
                                       start=True, stop=True)
                    mm.then_inc(lg_done, 1)

            pe.wait_ge(wraw_in, 48)
            for s in range(4):
                pe.transpose(s_ps[:, 2 * s:2 * s + 2, :], raw[:, s, :], ident)
            pe.transpose(y_ps[:, 0, 0:E * FC], raw[0:E * FC, 4, :], kc[0:E * FC, K_ID:K_ID + E * FC]).then_inc(wT_done, 1)

            def route_counts(k):
                if k == 2:
                    pe.wait_ge(route, ROUTE_BOTH)
                    pe.matmul(y_ps[:, 0:2, :], kc[:, K_TRI:K_TRI + P], both[:, :, :], start=True, stop=True)
                    pe.matmul(y_ps[:, 2:4, :], kc[:, K_ONE:K_ONE + P], both[:, :, :], start=True, stop=True).then_inc(counted, 1)
                    pe.wait_ge(route, ROUTE_READ)

            def attention(n, b, has):
                b, a = b % 2, 1 - b % 2
                if has(0):
                    wait_from(pe, prod_done, n)
                    for s in range(4):
                        mm = pe.matmul(qk_ps[:, s, :], wqk[:, s, :], xnT[:, bass.ds(n * P, P)], start=True, stop=True)
                    mm.then_inc(qk_done, 1)
                if has(1):
                    pe.wait_ge(qm_ready, n)
                    pe.wait_ge(kz_ready, n)
                    wait_from(pe, sub_done, n - 1)
                    for c in range(2):
                        cs = slice(CHUNK * c, CHUNK * (c + 1))
                        for j in range(NJ):
                            mm = pe.matmul(s_ps[cs, NG * j:NG * (j + 1), :], qm[:, a, j, cs], kz[:, a, :, cs],
                                           start=True, stop=True)
                    mm.then_inc(s_done, 1)
                if has(2):
                    pe.wait_ge(xv_ready, n - 1)
                    wait_from(pe, vbd_ready, n - 2)
                    for c in range(2):
                        mm = pe.matmul(v_ps[:, c, :], xv[:, b, c, :, :].rearrange("p r t -> p (r t)"), wv[:, :],
                                       start=True, stop=True)
                    mm.then_inc(v_done, 1)
                    pe.wait_ge(exp_done, n - 1)
                    wait_from(pe, pT_ready, n - 2)
                    for s in range(8):
                        mm = pe.transpose(t_ps[:, s, :], pr[:, b, 2 * s:2 * s + 2, :].rearrange("p h k -> p (h k)"), ident)
                    mm.then_inc(t_done, 1)
                if has(3):
                    pe.wait_ge(rexp_ready, n - 2)
                    wait_from(pe, rT_ready, n - 3)
                    wait_from(pe, acc_done, n - 4)
                    pe.transpose(m_ps[:, 0, :], rexp[:, :, :, :].rearrange("p g j d -> p (g j d)"), ident).then_inc(rT_done, 1)
                    pe.wait_ge(pT_ready, n - 2)
                    pe.wait_ge(vbd_ready, n - 2)
                    wait_from(pe, yT_ready, n - 3)
                    for g in range(2):
                        for c in range(2):
                            for j in range(NJ):
                                mm = pe.matmul(y_ps[CHUNK * g:CHUNK * (g + 1), c, :], vbd[:, a, c, g, 2 * GRP * j:2 * GRP * (j + 1)],
                                               pT[:, a, 2 * j + g, :], start=(j == 0), stop=(j == NJ - 1))
                    mm.then_inc(y_done, 1)
                if has(4):
                    pe.wait_ge(yT_ready, n - 3)
                    pe.wait_ge(rT_ready, n - 2 if has(3) else n - 3)
                    if not has(3):
                        pe.wait_ge(acc_done, n - 4)
                    pe.matmul(m_ps[:, 1, :], yT[:, b, :], wp[:, :], start=True, stop=True).then_inc(o_done, 1)

            def experts(n, b, has):
                u, b, a = b, b % 2, 1 - b % 2
                if has(0):
                    pe.wait_ge(xs_in[u // 2], (n - u) * 4 + 16)
                    wait_from(pe, xsT_ready, n)
                    pe.transpose(qk_ps[:, 0, :], xs[:, u, :], ident).then_inc(xsT_done, 1)
                if has(1):
                    pe.wait_ge(xsT_ready, n)
                    pe.wait_ge(wl1_ready, n)
                    wait_from(pe, hT_ready, n - 2)
                    for f in range(FC):
                        mm = pe.matmul(s_ps[:, 8 * a + 2 * f:8 * a + 2 * f + 2, :], wl1[:, a, f * P:(f + 1) * P], xsT[:, a, :],
                                       start=True, stop=True)
                    mm.then_inc(h_done, 1)
                if has(2):
                    pe.wait_ge(hT_ready, n - 1)
                    pe.wait_ge(wl2_ready, n - 1)
                    wait_from(pe, ys_ready, n - 2)
                    for f in range(FC):
                        mm = pe.matmul(v_ps[:, 0, :], hT[:, b, f, :], wl2[:, b, f * C:(f + 1) * C],
                                       start=(f == 0), stop=(f == FC - 1))
                    mm.then_inc(yy_done, 1)

            def first_attention(n, b, has):
                if at(n, 0):
                    pe.wait_ge(wT_copied, WT_COPIES)
                    pe.wait_ge(lg_ready, TILES // 4)
                attention(n, b, has)

            def experts_between(n, b, has):
                if at(n, 0):
                    pe.wait_ge(prod_done, HALF)
                if at(n, 1):
                    pe.wait_ge(sub_done, HALF)
                if at(n, 2):
                    pe.wait_ge(vbd_ready, HALF)
                experts(n, b, has)

            def second_attention(n, b, has):
                if at(n, HALF):
                    pe.wait_ge(xsT_ready, SLOT_TILES)
                if at(n, HALF + 1):
                    pe.wait_ge(hT_ready, SLOT_TILES)
                if at(n, HALF + 2):
                    pe.wait_ge(ys_ready, SLOT_TILES)
                attention(n, b, has)

            everything(pe, first_attention, experts_between, second_attention, route_counts)

        @block.scalar
        def _(act):
            for g in range(TILES // 4):
                act.wait_ge(xnT_done, g + 1)
                act.copy(xnT[:, 4 * g * P:4 * (g + 1) * P].rearrange("p (u t) -> p u t", u=4),
                         t_ps[:, 4 * (g % 2):4 * (g % 2) + 4, :]).then_inc(xnT_ready, 1)

            act.wait_ge(wT_done, 1)
            for s, to in enumerate((wqk[:, 0, :], wqk[:, 1, :], wv[:, :], wp[:, :])):
                act.copy(to.rearrange("p (a c) -> p a c", a=2), s_ps[:, 2 * s:2 * s + 2, :]).then_inc(wT_copied, 1)
            for s in range(2):
                src = s_ps[:, 2 * s:2 * s + 2, :].rearrange("p a (h u d) -> p (a h) u d", u=2, d=HD // 2)
                dst = wqk[:, 2 + s, :].rearrange("p (h u d) -> p h u d", u=2, d=HD // 2)
                for u in range(2):
                    act.copy(dst[:, :, u, :], src[:, :, 1 - u, :]).then_inc(wT_copied, 1)
            act.copy(wall[:, :, W_B1:W_2], y_ps[:, 0, 0:E * FC].rearrange("p (e f) -> p e f", e=E)).then_inc(wT_copied, 1)

            def route_exp(k):
                if k == 3:
                    act.wait_ge(gap_ready, 1)
                    act.activation(den[:, :], gap[:, :], ACT.Exp).then_inc(gap_exp, 1)

            def attention(n, b, has):
                b, a = b % 2, 1 - b % 2
                if has(0):
                    act.wait_ge(rot_done, n + 1)
                    wait_from(act, s_done, n - 1)
                    for g in range(NG):
                        gs = slice(GRP * g, GRP * (g + 1))
                        ins = act.copy(kz[gs, b, g, :], rot[gs, 1, :])
                    ins.then_inc(kz_ready, 1)
                    for j in range(NJ):
                        ins = act.activation(qm[:, b, j, :], rot[:, 0, :], ACT.Copy, scale=kc[:, K_MASK + j:K_MASK + j + 1])
                    ins.then_inc(qm_ready, 1)
                if has(1):
                    wait_from(act, v_done, n - 2)
                    act.copy(xv[:, a, :, :, :],
                             xnT[:, bass.ds((n - 1) * P, P)].rearrange("p (c r t) -> p c r t", c=2, r=1)
                             .to_broadcast([P, 2, 2, CHUNK])).then_inc(xv_ready, 1)
                if has(2):
                    act.wait_ge(v_done, n - 1)
                    wait_from(act, y_done, n - 3)
                    for c in range(2):
                        for r in range(2):
                            rs = slice(CHUNK * r, CHUNK * (r + 1))
                            src = v_ps[rs, c, :].rearrange("p (g r j d) -> p j g r d", g=2, r=2, j=NJ)[:, :, :, r, :]
                            dst = vbd[rs, b, c, :, :].rearrange("p g (j w) -> p j g w", j=NJ)[:, :, :, GRP * r:GRP * r + HD]
                            ins = act.copy(dst, src)
                    ins.then_inc(vbd_ready, 1)
                    act.wait_ge(t_done, n - 1)
                    wait_from(act, y_done, n - 3)
                    act.copy(pT[:, b, :, :], t_ps[:, :, :]).then_inc(pT_ready, 1)
                if has(3):
                    act.wait_ge(rT_done, n - 2)
                    wait_from(act, yT_ready, n - 3)
                    act.copy(rT[:, :], m_ps[:, 0, :]).then_inc(rT_ready, 1)
                if has(1):
                    act.wait_ge(sub_done, n)
                    act.activation(pr[:, a, :, :], pr[:, a, :, :], ACT.Exp, scale=SCALE).then_inc(exp_done, 1)

            def experts(n, b, has):
                b, a = b % 2, 1 - b % 2
                if has(1):
                    act.wait_ge(h_done, n)
                    wait_from(act, yy_done, n - 2)
                    for f in range(FC):
                        ins = act.activation(hT[:, a, f, :], s_ps[:, 8 * a + 2 * f:8 * a + 2 * f + 2, :].rearrange("p a c -> p (a c)"),
                                             ACT.Gelu, bias=wl1[:, a, F + f:F + f + 1])
                    ins.then_inc(hT_ready, 1)

            act.wait_ge(fills, 3)
            everything(act, attention, experts, attention, route_exp)

        @block.vector
        def _(dve):
            dve.memset(wgate[:, :], 0.0).then_inc(wgate_ready, 1)
            dve.memset(zeros[:, :], 0.0).then_inc(fills, 1)
            dve.memset(kz[:, :, :, :], 0.0).then_inc(fills, 1)
            dve.memset(vbd[:, :, :, :, :], 0.0).then_inc(fills, 1)

            def row_stats(i):
                ts = slice(i * XPART, (i + 1) * XPART)
                dve.wait_ge(x_in[i], 16)
                for t in range(i * XPART, (i + 1) * XPART):
                    dve.bn_stats(stats[:, t, :], acc[:, t, :]).then_inc(stats_done, 1)
                for t in range(i * XPART, (i + 1) * XPART):
                    dve.wait_ge(stats_done, t + 1)
                    dve.bn_aggr(mv[:, t, :], stats[:, t, :]).then_inc(mv_done, 1)
                dve.wait_ge(mv_done, (i + 1) * XPART)
                dve.tensor_scalar(var[:, ts], mv[:, ts, 1], EPS, None, ALU.add).then_inc(var_ready, 1)

            def normalise(i):
                dve.wait_ge(rstd_ready, i + 1)
                for t in range(i * XPART, (i + 1) * XPART):
                    ins = dve.tensor_scalar(xn[:, t, :], acc[:, t, :], mv[:, t, 0:1], rstd[:, t:t + 1], ALU.subtract, ALU.mult)
                ins.then_inc(xn_ready, 1)

            def keep_logits(g):
                dve.wait_ge(lg_done, g + 1)
                dve.tensor_tensor(lg[:, 4 * g:4 * g + 4, :], (m_ps if g % 2 else v_ps)[:, :, 0:E],
                                  gbias[:, :].rearrange("p (a e) -> p a e", a=1).to_broadcast([P, 4, E]),
                                  ALU.add).then_inc(lg_ready, 1)

            for i in range(6):
                if i < 4:
                    row_stats(i)
                if 1 <= i < 5:
                    normalise(i - 1)
                if i == 1:
                    dve.wait_ge(consts_in, 16)
                    for f in range(2):
                        for c in range(2):
                            src = kc[:, K_COS + f * CHUNK:K_COS + (f + 1) * CHUNK].rearrange("p (a t) -> p a t", a=1)
                            dve.tensor_copy(table[:, 2 * f:2 * f + 2, c * CHUNK:(c + 1) * CHUNK],
                                            src.to_broadcast([P, 2, CHUNK])).then_inc(table_ready, 1)
                    dve.wait_ge(gate_in, 32)
                if i >= 2:
                    keep_logits(2 * i - 4)
                    keep_logits(2 * i - 3)

            steps = [0]

            def then_route(ins):
                ins.then_inc(route, 1)
                steps[0] += 1
                dve.wait_ge(route, steps[0])

            def over_e(v):
                return v.rearrange("p (t a) -> p t a", a=1).to_broadcast([P, TILES, E])

            e8 = kc[:, K_E8:K_E8 + E].rearrange("p (a e) -> p a e", a=1).to_broadcast([P, TILES, E])

            def choose(k):
                then_route(dve.tensor_reduce(best[:, k, :], lg[:, :, :], AX.X, ALU.max))
                then_route(dve.tensor_tensor(work[:, :, :], lg[:, :, :], over_e(best[:, k, :]), ALU.is_equal))
                then_route(dve.tensor_tensor(work[:, :, :], work[:, :, :], e8, ALU.mult))
                then_route(dve.tensor_reduce(pick[:, k, :], work[:, :, :], AX.X, ALU.min))
                then_route(dve.tensor_tensor(hot[:, k, :, :], e8, over_e(pick[:, k, :]), ALU.is_equal))
                if k == 0:
                    then_route(dve.scalar_tensor_tensor(out=lg[:, :, :], in0=hot[:, 0, :, :], scalar=FAR, in1=lg[:, :, :],
                                                        op0=ALU.mult, op1=ALU.add))
                else:
                    then_route(dve.tensor_tensor(both[:, :, :].rearrange("p e t -> p t e"), hot[:, 0, :, :], hot[:, 1, :, :], ALU.add))
                    assert steps[0] == ROUTE_BOTH
                    dve.tensor_tensor(gap[:, :], best[:, 1, :], best[:, 0, :], ALU.subtract).then_inc(gap_ready, 1)

            total = y_ps[:, 2:4, :].rearrange("p a c -> p (a c)")
            run_e = run[:, :].rearrange("p (e t) -> p e t", e=E)
            def count_pairs():
                dve.wait_ge(counted, 1)
                then_route(dve.tensor_copy(place[:, :, :].rearrange("p e t -> p (e t)"), total))
                then_route(dve.tensor_tensor_scan(run[:, :], kc[:, K_ONE:K_ONE + 1].to_broadcast([P, E * TILES]),
                                                  place[:, :, :].rearrange("p e t -> p (e t)"), 0.0, ALU.mult, ALU.add))
                then_route(dve.tensor_tensor(place[:, :, :], run_e, place[:, :, :], ALU.subtract))
                then_route(dve.tensor_tensor(place[:, :, :].rearrange("p e t -> p (e t)"), place[:, :, :].rearrange("p e t -> p (e t)"),
                                             y_ps[:, 0:2, :].rearrange("p a c -> p (a c)"), ALU.add))
                assert steps[0] == ROUTE_READ

            def lay_out():
                then_route(dve.tensor_copy(load_e[:, 0:1], run_e[:, 0, TILES - 1:TILES]))
                then_route(dve.tensor_tensor(load_e[:, 1:E], run_e[:, 1:E, TILES - 1], run_e[:, 0:E - 1, TILES - 1], ALU.subtract))
                then_route(dve.tensor_tensor(many[:, :, :], load_e[:, :].rearrange("p (e a) -> p e a", a=1).to_broadcast([P, E, TILES]),
                                             kc[:, K_STEP:K_STEP + TILES].rearrange("p (a t) -> p a t", a=1).to_broadcast([P, E, TILES]),
                                             ALU.is_gt))
                then_route(dve.tensor_reduce(padded[:, :], many[:, :, :], AX.X, ALU.add))
                then_route(dve.tensor_scalar(padded[:, :], padded[:, :], float(P), None, ALU.mult))
                then_route(dve.tensor_tensor_scan(ends[:, :], kc[:, K_ONE:K_ONE + 1].to_broadcast([P, E]), padded[:, :], 0.0,
                                                  ALU.mult, ALU.add))
                then_route(dve.tensor_tensor(shift[:, :], ends[:, :], padded[:, :], ALU.subtract))
                then_route(dve.tensor_tensor(shift[:, :], shift[:, :], run_e[:, :, TILES - 1], ALU.subtract))
                then_route(dve.tensor_tensor(shift[:, :], shift[:, :], load_e[:, :], ALU.add))

            def find_places():
                then_route(dve.tensor_tensor(place[:, :, :], place[:, :, :],
                                             shift[:, :].rearrange("p (e a) -> p e a", a=1).to_broadcast([P, E, TILES]), ALU.add))
                for k in range(2):
                    then_route(dve.tensor_tensor(work[:, :, :], hot[:, k, :, :], place[:, :, :].rearrange("p e t -> p t e"), ALU.mult))
                    then_route(dve.tensor_reduce(posf[:, k, :], work[:, :, :], AX.X, ALU.add))
                dve.tensor_copy(pos[:, :, :], posf[:, :, :]).then_inc(pos_ready, 1)

            def tiles_and_weights():
                then_route(dve.tensor_tensor(late[:, :, :],
                                             kc[0:1, K_START:K_START + SLOT_TILES].rearrange("p (t a) -> p t a", a=1).to_broadcast([1, SLOT_TILES, E]),
                                             ends[0:1, :].rearrange("p (a e) -> p a e", a=1).to_broadcast([1, SLOT_TILES, E]), ALU.is_ge))
                then_route(dve.tensor_reduce(eidf[:, :], late[:, :, :], AX.X, ALU.add))
                then_route(dve.tensor_scalar(eidf[:, :], eidf[:, :], float(E - 1), None, ALU.min))
                dve.tensor_copy(eid[:, :], eidf[:, :]).then_inc(eid_ready, 1)
                dve.wait_ge(gap_exp, 1)
                then_route(dve.tensor_scalar(wt[:, 1, :], den[:, :], 1.0, None, ALU.add))
                then_route(dve.reciprocal(wt[:, 0, :], wt[:, 1, :]))
                assert steps[0] == ROUTE_END - 1
                then_route(dve.tensor_tensor(wt[:, 1, :], den[:, :], wt[:, 0, :], ALU.mult))

            def route_part(k):
                if k < 2:
                    choose(k)
                if k == 2:
                    count_pairs()
                if k == 3:
                    lay_out()
                if k == 4:
                    find_places()
                if k == 5:
                    tiles_and_weights()

            def attention(n, b, has):
                b, a = b % 2, 1 - b % 2
                if has(0):
                    dve.wait_ge(qk_done, n + 1)
                    wait_from(dve, rot_done, n)
                    dve.tensor_tensor(rp[:, :, :], qk_ps[:, :, :], table[:, :, :], ALU.mult).then_inc(prod_done, 1)
                    dve.wait_ge(prod_done, n + 1)
                    wait_from(dve, kz_ready, n)
                    wait_from(dve, qm_ready, n)
                    dve.tensor_tensor(rot[:, :, :], rp[:, 0:2, :], rp[:, 2:4, :], ALU.add).then_inc(rot_done, 1)
                if has(1):
                    dve.wait_ge(s_done, n)
                    wait_from(dve, sub_done, n - 1)
                    dve.tensor_reduce(mx[:, :], s_ps[:, :, :], AX.X, ALU.max).then_inc(max_done, 1)
                    dve.wait_ge(max_done, n)
                    wait_from(dve, t_done, n - 2)
                    wait_from(dve, sum_done, n - 2)
                    dve.tensor_tensor(pr[:, a, :, :], s_ps[:, :, :],
                                      mx[:, :].rearrange("p (h a) -> p h a", a=1).to_broadcast([P, NJ * NG, CHUNK]),
                                      ALU.subtract).then_inc(sub_done, 1)
                if has(2):
                    dve.wait_ge(exp_done, n - 1)
                    wait_from(dve, rc_done, n - 2)
                    dve.tensor_reduce(sm[:, :], pr[:, b, :, :], AX.X, ALU.add).then_inc(sum_done, 1)
                    dve.wait_ge(sum_done, n - 1)
                    wait_from(dve, rexp_ready, n - 2)
                    dve.reciprocal(rc[:, :], sm[:, :]).then_inc(rc_done, 1)
                    dve.wait_ge(rc_done, n - 1)
                    wait_from(dve, rT_done, n - 2)
                    dve.tensor_copy(rexp[:, :, :, :].rearrange("p g j d -> p j g d"),
                                    rc[:, :].rearrange("p (j g a) -> p j g a", j=NJ, a=1).to_broadcast([P, NJ, NG, HD])
                                    ).then_inc(rexp_ready, 1)
                if has(3):
                    dve.wait_ge(y_done, n - 2)
                    dve.wait_ge(rT_ready, n - 2)
                    wait_from(dve, o_done, n - 4)
                    for c in range(2):
                        cs = slice(CHUNK * c, CHUNK * (c + 1))
                        ins = dve.tensor_tensor(yT[:, a, cs], y_ps[:, c, cs], rT[:, cs], ALU.mult)
                    ins.then_inc(yT_ready, 1)
                if has(4):
                    dve.wait_ge(o_done, n - 3)
                    dve.tensor_tensor(acc[:, bass.ds(n - 4, 1), :], acc[:, bass.ds(n - 4, 1), :], m_ps[:, 1:2, :],
                                      ALU.add).then_inc(acc_done, 1)

            def combine(m, b, t0):
                dve.wait_ge(gathered[b], (m - b) * (PAIR // 2) + PAIR)
                for k in range(TOP_K):
                    for u in range(2):
                        here = acc[:, bass.ds(t0 + u, 1), :]
                        ins = dve.scalar_tensor_tensor(out=here, in0=got[:, k, bass.ds(t0 + u, 1), :],
                                                       scalar=wt[:, k, bass.ds(t0 + u, 1)], in1=here,
                                                       op0=ALU.mult, op1=ALU.add)
                        ins.then_inc(part_done if k == 0 else tile_done, 1)
                    if k == 0:
                        dve.wait_ge(part_done, (m + 1) * 2)

            def attention_and_combine(n, b, has):
                attention(n, b, has)
                if has(4):
                    dve.wait_ge(acc_done, n - 3)
                    combine(n - (4 + HALF), b % 2, (n - (4 + HALF)) * 2)

            def expert_of(n):
                return nc.vector.value_load(eid[0:1, bass.ds(n, 1)], min_val=0, max_val=E - 1)

            def experts(n, b, has):
                u, b, a = b, b % 2, 1 - b % 2
                if has(0):
                    e = expert_of(n)
                    dve.wait_ge(xsT_done, n + 1)
                    wait_from(dve, h_done, n - 1)
                    dve.tensor_copy(xsT[:, b, :], qk_ps[:, 0, :]).then_inc(xsT_ready, 1)
                    wait_from(dve, hT_ready, n - 1)
                    dve.tensor_copy(wl1[:, b:b + 1, :], wall[:, bass.ds(e, 1), 0:W_2]).then_inc(wl1_ready, 1)
                if has(1):
                    e = expert_of(n - 1)
                    wait_from(dve, yy_done, n - 2)
                    wait_from(dve, ys_ready, n - 2)
                    dve.tensor_copy(wl2[:, a:a + 1, :], wall[:, bass.ds(e, 1), W_2:W_ALL]).then_inc(wl2_ready, 1)
                if has(2):
                    dve.wait_ge(yy_done, n - 1)
                    w = (u + 2) % RING
                    wait_from(dve, ys_out[w // 2], (n - (2 + w)) * 4)
                    dve.tensor_tensor(ys[:, w, :], v_ps[:, 0, :], wl2[:, b, FC * C:FC * C + C], ALU.add).then_inc(ys_ready, 1)

            def experts_between(n, b, has):
                if at(n, 0):
                    dve.wait_ge(wall_in, 16 * (E + 2))
                    dve.wait_ge(wT_copied, WT_COPIES)
                    dve.wait_ge(eid_ready, 1)
                experts(n, b, has)

            def first_attention(n, b, has):
                if at(n, 0):
                    dve.wait_ge(table_ready, 4)
                attention(n, b, has)

            everything(dve, first_attention, experts_between, attention_and_combine, route_part)


ROUTE_BOTH = 12
ROUTE_READ = ROUTE_BOTH + 4
ROUTE_END = ROUTE_READ + 10 + 4 + 3 + 3
WT_COPIES = 9

_INS = ["L0_attn_x", "L0_attn_w_attn", "L0_attn_w_proj", "L0_ffn_gate_w", "L0_ffn_gate_b",
        "L0_ffn_w1", "L0_ffn_b1", "L0_ffn_w2", "L0_ffn_b2"]


def kernel(**inputs):
    import concourse.bacc as bacc
    from concourse.bass_utils import run_bass_kernel_spmd

    nc = bacc.Bacc("TRN2", target_bir_lowering=False, num_devices=1)
    arrays = {"in_" + n: np.ascontiguousarray(inputs[n]) for n in _INS}
    arrays["in_consts"] = constants()
    aps = [nc.dram_tensor(n, a.shape, mybir.dt.from_np(a.dtype), kind="ExternalInput").ap() for n, a in arrays.items()]
    out = nc.dram_tensor("out_0", (BATCH, SEQ, C), F32, kind="ExternalOutput").ap()
    build(nc, *aps, out)
    r = run_bass_kernel_spmd(nc, [arrays], core_ids=[0])
    return r.results[0]["out_0"]
```

```python
from contextlib import ExitStack

import numpy as np

import concourse.bass as bass
from concourse import mybir

F32 = mybir.dt.float32
I32 = mybir.dt.int32
ALU = mybir.AluOpType
ACT = mybir.ActivationFunctionType
AX = mybir.AxisListType

P = 128
BATCH, SEQ, C = 2, 2048, 128
TOKENS = BATCH * SEQ
TILES = TOKENS // P
HALF = TILES // 2
HEADS, CHUNK = 16, 64
HD = C // HEADS
NJ, NG = 4, 4
GRP = NJ * HD
DIAG = 2 * GRP + HD
SWAP = [i // HD * HD + (i + HD // 2) % HD for i in range(GRP)]
SCALE = 1.0 / float(np.sqrt(HD))
ROPE_BASE = 10000.0
EPS = 1e-5
E, F, TOP_K = 8, 512, 2
FC = F // P
SLOT_TILES = TOKENS * TOP_K // P + E
SLOTS = SLOT_TILES * P
ROW = C + 1
FAR = -3.0e38

K_ID, K_COS, K_SIN, K_MASK = 0, P, P + CHUNK, P + 2 * CHUNK
K_TRI = K_MASK + NJ
K_ONE = K_TRI + P
K_E8 = K_ONE + P
K_STEP = K_E8 + E
K_START = K_STEP + TILES
K_ALL = K_START + SLOT_TILES

W_B1, W_2, W_B2 = F, F + FC, F + FC + FC * C
W_ALL = W_B2 + C


def constants():
    k = np.zeros((P, K_ALL), np.float32)
    k[:, K_ID:K_ID + P] = np.eye(P)
    row = np.arange(P)
    d = row % HD
    freq = (np.float32(1.0) / np.float32(ROPE_BASE) ** (np.arange(0, HD, 2, dtype=np.float32) / np.float32(HD))).astype(np.float32)
    angle = np.outer(freq[d % (HD // 2)], np.arange(CHUNK, dtype=np.float32)).astype(np.float32)
    k[:, K_COS:K_COS + CHUNK] = np.cos(angle)
    k[:, K_SIN:K_SIN + CHUNK] = np.sin(angle) * np.where(d < HD // 2, -1.0, 1.0)[:, None]
    for j in range(NJ):
        k[:, K_MASK + j] = (row // HD) % NJ == j
    k[:, K_TRI:K_TRI + P] = row[:, None] < row[None, :]
    k[:, K_ONE:K_ONE + P] = 1.0
    k[:, K_E8:K_E8 + E] = np.arange(E) - E
    k[:, K_STEP:K_STEP + TILES] = np.arange(TILES) * P
    k[:, K_START:K_START + SLOT_TILES] = np.arange(SLOT_TILES) * P
    return k


def build(nc, x, w_attn, w_proj, gate_w, gate_b, w1, b1, w2, b2, consts, out):
    with ExitStack() as ctx:
        def sb(name, shape, dt=F32):
            return ctx.enter_context(nc.sbuf_tensor("sb_" + name, shape, dt))

        def sem(name):
            return ctx.enter_context(nc.semaphore(name))

        xg_dram = nc.dram_tensor("slot_rows", [SLOTS, ROW], F32).ap()
        yg_dram = nc.dram_tensor("slot_results", [SLOTS, C], F32).ap()

        kc = sb("consts", [P, K_ALL])
        acc = sb("acc", [P, TILES, C])
        xn = sb("xn", [P, TILES, ROW])
        xnT = sb("xnT", [P, TOKENS])
        wall = sb("expert_weights", [P, E, W_ALL])
        wqk = sb("wqk", [P, 2, P])
        wv = sb("wv", [P, P])
        wp = sb("wp", [P, P])
        raw = sb("raw_weights", [P, 5, P])
        wgate = sb("wgate", [P, P])
        gbias = sb("gbias", [P, E])
        zeros = sb("zeros", [P, ROW])
        table = sb("rope_table", [P, 4, P])

        stats = sb("stats", [P, TILES, 6])
        mv = sb("mv", [P, TILES, 2])
        var = sb("var", [P, TILES])
        power = sb("power", [P, TILES])
        rstd = sb("rstd", [P, TILES])
        nmean = sb("nmean", [P, TILES])
        mshift = sb("mshift", [P, TILES])

        lg = sb("logits", [P, TILES, E])
        best = sb("best", [P, 2, TILES])
        pick = sb("pick", [P, 2, TILES])
        work = sb("work", [P, TILES, E])
        hot = sb("hot", [P, 2, TILES, E])
        both = sb("both", [P, E, TILES])
        run = sb("run", [P, E * TILES])
        place = sb("place", [P, E, TILES])
        load_e = sb("load_e", [P, E])
        many = sb("many", [P, E, TILES])
        padded = sb("padded", [P, E])
        ends = sb("ends", [P, E])
        shift = sb("shift", [P, E])
        posf = sb("posf", [P, 2, TILES])
        pos = sb("pos", [P, 2, TILES], I32)
        late = sb("late", [1, SLOT_TILES, E])
        eidf = sb("eidf", [1, SLOT_TILES])
        eid = sb("eid", [1, SLOT_TILES], I32)
        gap = sb("gap", [P, TILES])
        den = sb("den", [P, TILES])
        den1 = sb("den1", [P, TILES])
        wt2 = sb("wt2", [P, TILES])

        rp = sb("rope_products", [P, 4, P])
        sw = sb("sw", [P, 2, P])
        rot = sb("rot", [P, 2, P])
        qm = sb("qm", [P, 2, NJ, P])
        kz = sb("kz", [P, 2, NG, P])
        xv = sb("xv", [P, 2, 2, 2, CHUNK])
        vbd = sb("vbd", [P, 2, 2, 2, NJ * DIAG])
        pr = sb("probs", [P, 2, NJ * NG, CHUNK])
        pT = sb("probsT", [P, 2, NJ * 2, P])
        mx = sb("mx", [P, NJ * NG])
        sm = sb("sm", [P, NJ * NG])
        rc = sb("rc", [P, NJ * NG])
        rexp = sb("rexp", [P, NG, NJ, HD])
        rT = sb("rT", [P, P])
        yT = sb("yT", [P, 2, P])

        xs = sb("xs", [P, 4, ROW])
        slot_w = sb("slot_w", [P, 4])
        xsT = sb("xsT", [P, 2, P])
        wl = sb("wl", [P, 4, W_ALL])
        hT = sb("hT", [P, 2, FC, P])
        ys = sb("ys", [P, 4, P])
        got = [xn[:, :, 0:C], sb("got", [P, TILES, C])[:, :, :]]

        qk_ps = ctx.enter_context(nc.psum_tensor("qk_ps", [P, 4, P], F32))
        v_ps = ctx.enter_context(nc.psum_tensor("v_ps", [P, 4, P], F32))
        s_ps = ctx.enter_context(nc.psum_tensor("s_ps", [P, NJ * NG, CHUNK], F32))
        t_ps = ctx.enter_context(nc.psum_tensor("t_ps", [P, 8, P], F32))
        y_ps = ctx.enter_context(nc.psum_tensor("y_ps", [P, 4, P], F32))
        m_ps = ctx.enter_context(nc.psum_tensor("m_ps", [P, 4, P], F32))

        x_in = [sem(f"x_in{i}") for i in range(4)]
        consts_in, wraw_in, gate_in, wall_in = sem("consts_in"), sem("wraw_in"), sem("gate_in"), sem("wall_in")
        fills, wgate_ready, wT_done, wT_copied, table_ready = (
            sem("fills"), sem("wgate_ready"), sem("wT_done"), sem("wT_copied"), sem("table_ready"))
        stats_done, mv_done, power_ready, var_ready, rstd_ready, mshift_ready = (
            sem("stats_done"), sem("mv_done"), sem("power_ready"), sem("var_ready"), sem("rstd_ready"),
            sem("mshift_ready"))
        xn_ready, xnT_done, xnT_ready, lg_done, lg_ready = (
            sem("xn_ready"), sem("xnT_done"), sem("xnT_ready"), sem("lg_done"), sem("lg_ready"))
        route, counted, gap_ready, gap_exp, pos_ready, eid_ready = (
            sem("route"), sem("counted"), sem("gap_ready"), sem("gap_exp"), sem("pos_ready"),
            sem("eid_ready"))
        zeroed, second_weights = sem("zeroed"), sem("second_weights")
        scattered = [sem(f"scattered{h}") for h in range(2)]
        qk_done, sines_done, prod_done, sw_done, rot_done, qm_ready, kz_ready, xv_ready = (
            sem("qk_done"), sem("sines_done"), sem("prod_done"), sem("sw_done"), sem("rot_done"), sem("qm_ready"), sem("kz_ready"), sem("xv_ready"))
        v_done, vbd_ready, s_done, max_done, sub_done, exp_done = (
            sem("v_done"), sem("vbd_ready"), sem("s_done"), sem("max_done"), sem("sub_done"), sem("exp_done"))
        sum_done, rc_done, rexp_ready, rT_done, rT_ready = (
            sem("sum_done"), sem("rc_done"), sem("rexp_ready"), sem("rT_done"), sem("rT_ready"))
        t_done, pT_ready, y_done, yT_ready, o_done, acc_done = (
            sem("t_done"), sem("pT_ready"), sem("y_done"), sem("yT_ready"), sem("o_done"), sem("acc_done"))
        xs_in = [sem(f"xs_in{b}") for b in range(2)]
        xsT_done, xsT_ready, wl_ready = sem("xsT_done"), sem("xsT_ready"), sem("wl_ready")
        slot_w_ready, biased = sem("slot_w_ready"), sem("biased")
        h_done, hT_ready, yy_done, ys_ready = (
            sem("h_done"), sem("hT_ready"), sem("yy_done"), sem("ys_ready"))
        ys_out = [sem(f"ys_out{b}") for b in range(2)]
        gathered = [sem(f"gathered{b}") for b in range(2)]
        part_done, tile_done, out_done = sem("part_done"), sem("tile_done"), sem("out_done")

        lg_ps = y_ps[:, :, :].rearrange("p a c -> p (a c)")

        XPART = TILES // 4
        PAIR = 16 * 2 * TOP_K

        def at(n, k):
            return isinstance(n, int) and n == k

        def steady(eng, step, first, end, unroll):
            assert (end - first) % unroll == 0
            with eng.Fori(0, (end - first) // unroll, 1) as i:
                for b in range(unroll):
                    step(i * unroll + (first + b), (first + b) % RING, lambda s: True)

        def tail(step, end, first, count):
            for n in range(first, first + count):
                step(n, n % RING, lambda s, n=n: n - s < end)

        def everything(eng, attention, experts, second_attention, between):
            for k in range(HEAD):
                attention(k, k % RING, lambda s: k - s >= 0)
                between(k)
            steady(eng, attention, HEAD, HALF, 2)
            k = 0
            for i, share in enumerate(HEAD_SHARES):
                tail(attention, HALF, HALF + i, 1)
                for k in range(k, k + share):
                    experts(k, k % RING, lambda s: k - s >= 0)
                k += 1
            steady(eng, experts, EXPERTS_HEAD, SLOT_TILES - RING, RING)
            k = SLOT_TILES - RING
            for i in range(HEAD):
                for k in range(k, k + TAIL_SHARES[i]):
                    tail(experts, SLOT_TILES, k, 1)
                k += TAIL_SHARES[i] > 0
                second_attention(HALF + i, (HALF + i) % RING, lambda s: i - s >= 0)
            steady(eng, second_attention, HALF + HEAD, TILES, 2)
            tail(second_attention, TILES, TILES, LAG)

        def wait_from(eng, semaphore, value):
            if not isinstance(value, int) or value > 0:
                eng.wait_ge(semaphore, value)

        RING = 4
        LAG, EXPERTS_LAG = 5, 3
        HEAD, EXPERTS_HEAD = 6, 12
        HEAD_SHARES = (1, 2, 2, 2, 5)
        TAIL_SHARES = (4, 1, 1, 1, 0, 0)
        EARLY = 8
        assert len(HEAD_SHARES) == LAG and sum(HEAD_SHARES) == EXPERTS_HEAD >= EARLY + EXPERTS_LAG
        assert sum(TAIL_SHARES) == RING + EXPERTS_LAG and EARLY > sum(HEAD_SHARES[:-1])

        def early(n, s):
            return isinstance(n, int) and n - s < EARLY

        def row_bank(n):
            return qk_ps if early(n, 0) else m_ps

        def hidden_bank(n, a, f):
            if early(n, 1):
                return s_ps[:, 8 * a + 2 * f:8 * a + 2 * f + 2, :].rearrange("p a c -> p (a c)")
            return t_ps[:, 4 * a + f, :]

        def result_bank(n):
            return v_ps if early(n, 2) else y_ps

        block = ctx.enter_context(nc.Block())

        @block.sync
        def _(sp):
            x_t = x.rearrange("b (t p) c -> p (b t) c", p=P)
            out_t = out.rearrange("b (t p) c -> p (b t) c", p=P)
            def load_x(i):
                sp.dma_start(acc[:, i * XPART:(i + 1) * XPART, :], x_t[:, i * XPART:(i + 1) * XPART, :]).then_inc(x_in[i], 16)

            load_x(0)
            sp.dma_start(kc[:, :], consts).then_inc(consts_in, 16)
            load_x(1)
            load_x(2)
            sp.wait_ge(wgate_ready, 1)
            sp.dma_start(wgate[:, 0:E], gate_w).then_inc(gate_in, 16)
            sp.dma_start(gbias[:, :], gate_b.rearrange("(a e) -> a e", a=1).partition_broadcast(P)
                         .rearrange("p a e -> p (a e)")).then_inc(gate_in, 16)
            load_x(3)
            sp.dma_start(raw[:, 0:3, :], w_attn.rearrange("(s o) c -> o s c", s=3)).then_inc(wraw_in, 16)
            sp.dma_start(raw[:, 3, :], w_proj).then_inc(wraw_in, 16)
            sp.dma_start(raw[0:E * FC, 4, :], b1.rearrange("e (f p) -> (e f) p", p=P)).then_inc(wraw_in, 16)
            sp.wait_ge(fills, 1)
            sp.dma_start(xg_dram.rearrange("(t p) c -> p t c", p=P),
                         zeros[:, :].rearrange("p (a c) -> p a c", a=1).to_broadcast([P, SLOT_TILES, ROW])).then_inc(zeroed, 16)
            sp.dma_start(wall[:, :, 0:F], w1.rearrange("e c f -> c e f")).then_inc(wall_in, 16)
            for e in range(E):
                sp.dma_start(wall[:, e, W_2:W_B2].rearrange("p (k d) -> p k d", k=FC),
                             w2[e].rearrange("(k p) d -> p k d", p=P)).then_inc(wall_in, 16)
            sp.dma_start(wall[:, :, W_B2:W_ALL], b2.rearrange("(a e) d -> a e d", a=1).partition_broadcast(P)
                         .rearrange("p a e d -> p (a e) d")).then_inc(wall_in, 16)

            xg_t = xg_dram.rearrange("(t p) c -> p t c", p=P)
            yg_t = yg_dram.rearrange("(t p) c -> p t c", p=P)

            def load_slots(m, b):
                sp.dma_start(xs[:, 2 * b:2 * b + 2, :], xg_t[:, bass.ds(m * 2, 2), :]).then_inc(xs_in[b], 16)

            def store_slots(m, b):
                sp.wait_ge(ys_ready, m * 2 + 2)
                sp.dma_start(yg_t[:, bass.ds(m * 2, 2), :], ys[:, 2 * b:2 * b + 2, :]).then_inc(ys_out[b], 16)

            for h in range(2):
                sp.wait_ge(scattered[h], 16 * TOP_K * HALF)
            for m in range(2):
                load_slots(m, m)
            def next_slots(m, b):
                sp.wait_ge(slot_w_ready, m * 2 - 2)
                load_slots(m, b)

            next_slots(2, 0)
            with sp.Fori(0, SLOT_TILES // 4 - 2, 1) as i:
                for b in range(2):
                    next_slots(i * 2 + (b + 3), 1 - b)
                    store_slots(i * 2 + b, b)
            next_slots(SLOT_TILES // 2 - 1, 1)
            for m in range(SLOT_TILES // 2 - 4, SLOT_TILES // 2):
                store_slots(m, m % 2)

            with sp.Fori(0, TILES // 2, 1) as i:
                sp.wait_ge(tile_done, i + 1)
                sp.dma_start(out_t[:, bass.ds(i * 2, 2), :], acc[:, bass.ds(i * 2, 2), :]).then_inc(out_done, 16)
            sp.wait_ge(out_done, 16 * (TILES // 2))

        @block.gpsimd
        def _(pool):
            pool.memset(power[:, :], -0.5).then_inc(power_ready, 1)
            pool.wait_ge(power_ready, 1)
            for i in range(4):
                ts = slice(i * XPART, (i + 1) * XPART)
                pool.wait_ge(var_ready, i + 1)
                pool.tensor_tensor(rstd[:, ts], var[:, ts], power[:, ts], ALU.pow).then_inc(rstd_ready, 1)
                pool.wait_ge(rstd_ready, i + 1)
                pool.tensor_tensor(mshift[:, ts], nmean[:, ts], rstd[:, ts], ALU.mult).then_inc(mshift_ready, 1)

            pool.wait_ge(pos_ready, 1)
            pool.wait_ge(zeroed, 16)
            pool.wait_ge(xn_ready, TILES)
            pool.wait_ge(route, ROUTE_WEIGHTS)

            def scatter(k, h):
                for t in range(h * HALF, (h + 1) * HALF):
                    pool.indirect_dma_start(xg_dram, bass.IndirectOffsetOnAxis(ap=pos[:, k, t:t + 1], axis=0),
                                            xn[:, t, :], None).then_inc(scattered[h], 16)

            for h in range(2):
                scatter(0, h)
            for h in range(2):
                pool.wait_ge(scattered[h], 16 * HALF)
                pool.tensor_copy(xn[:, h * HALF:(h + 1) * HALF, C:ROW],
                                 wt2[:, h * HALF:(h + 1) * HALF].rearrange("p (t a) -> p t a", a=1)).then_inc(second_weights, 1)
                pool.wait_ge(second_weights, h + 1)
                scatter(1, h)

            for b in range(2):
                pool.wait_ge(ys_out[b], 16 * (SLOT_TILES // 4))

            for h in range(2):
                pool.wait_ge(scattered[h], 16 * TOP_K * HALF)
            for t in range(TILES):
                m = t // 2
                if t % 2 == 0 and m >= 2:
                    pool.wait_ge(gathered[m % 2], PAIR * (m // 2))
                for k in range(TOP_K):
                    pool.indirect_dma_start(got[k][:, t, :], None, yg_dram,
                                            bass.IndirectOffsetOnAxis(ap=pos[:, k, t:t + 1], axis=0)).then_inc(gathered[m % 2], 16)

        @block.tensor
        def _(pe):
            ident = kc[:, K_ID:K_ID + P]
            pe.wait_ge(consts_in, 16)
            pe.wait_ge(gate_in, 32)

            for g in range(TILES // 4 + 1):
                if g < TILES // 4:
                    pe.wait_ge(xn_ready, 4 * g + 4)
                    wait_from(pe, xnT_ready, g - 1)
                    for u in range(4):
                        mm = pe.transpose(t_ps[:, 4 * (g % 2) + u, :], xn[:, 4 * g + u, 0:C], ident)
                    mm.then_inc(xnT_done, 1)
                if g >= 1:
                    pe.wait_ge(xnT_ready, g)
                    for u in range(4):
                        t = 4 * (g - 1) + u
                        mm = pe.matmul(lg_ps[:, t * E:t * E + P], xnT[:, t * P:(t + 1) * P], wgate[:, :],
                                       start=True, stop=True)
                    mm.then_inc(lg_done, 1)

            pe.wait_ge(wraw_in, 48)
            for s in range(4):
                pe.transpose(s_ps[:, 2 * s:2 * s + 2, :], raw[:, s, :], ident)
            pe.transpose(m_ps[:, 0, 0:E * FC], raw[0:E * FC, 4, :], kc[0:E * FC, K_ID:K_ID + E * FC]).then_inc(wT_done, 1)

            def route_counts(k):
                if k == 1:
                    pe.wait_ge(route, ROUTE_BOTH)
                    pe.matmul(y_ps[:, 0:2, :], kc[:, K_TRI:K_TRI + P], both[:, :, :], start=True, stop=True)
                    pe.matmul(y_ps[:, 2:4, :], kc[:, K_ONE:K_ONE + P], both[:, :, :], start=True, stop=True).then_inc(counted, 1)
                if k == 2:
                    pe.wait_ge(route, ROUTE_READ)

            def attention(n, b, has):
                b, a = b % 2, 1 - b % 2
                if has(0):
                    wait_from(pe, prod_done, n)
                    for s in range(2):
                        mm = pe.matmul(qk_ps[:, s, :], wqk[:, s, :], xnT[:, bass.ds(n * P, P)], start=True, stop=True)
                    mm.then_inc(qk_done, 1)
                if has(1):
                    pe.wait_ge(qm_ready, n)
                    pe.wait_ge(kz_ready, n)
                    wait_from(pe, sub_done, n - 1)
                    for c in range(2):
                        cs = slice(CHUNK * c, CHUNK * (c + 1))
                        for j in range(NJ):
                            mm = pe.matmul(s_ps[cs, NG * j:NG * (j + 1), :], qm[:, a, j, cs], kz[:, a, :, cs],
                                           start=True, stop=True)
                    mm.then_inc(s_done, 1)
                if has(2):
                    pe.wait_ge(xv_ready, n - 1)
                    wait_from(pe, vbd_ready, n - 2)
                    for c in range(2):
                        mm = pe.matmul(v_ps[:, c, :], xv[:, b, c, :, :].rearrange("p r t -> p (r t)"), wv[:, :],
                                       start=True, stop=True)
                    mm.then_inc(v_done, 1)
                    pe.wait_ge(exp_done, n - 1)
                    wait_from(pe, pT_ready, n - 2)
                    for s in range(8):
                        mm = pe.transpose(t_ps[:, s, :], pr[:, b, 2 * s:2 * s + 2, :].rearrange("p h k -> p (h k)"), ident)
                    mm.then_inc(t_done, 1)
                if has(3):
                    pe.wait_ge(pT_ready, n - 2)
                    pe.wait_ge(vbd_ready, n - 2)
                    wait_from(pe, yT_ready, n - 3)
                    for g in range(2):
                        for c in range(2):
                            for j in range(NJ):
                                mm = pe.matmul(y_ps[CHUNK * g:CHUNK * (g + 1), c, :], vbd[:, a, c, g, 2 * GRP * j:2 * GRP * (j + 1)],
                                               pT[:, a, 2 * j + g, :], start=(j == 0), stop=(j == NJ - 1))
                    mm.then_inc(y_done, 1)
                if has(4):
                    pe.wait_ge(yT_ready, n - 3)
                    wait_from(pe, acc_done, n - 4)
                    pe.matmul(m_ps[:, 1, :], yT[:, b, :], wp[:, :], start=True, stop=True).then_inc(o_done, 1)
                if has(3):
                    pe.wait_ge(rexp_ready, n - 2)
                    pe.transpose(m_ps[:, 0, :], rexp[:, :, :, :].rearrange("p g j d -> p (g j d)"), ident).then_inc(rT_done, 1)

            def experts(n, b, has):
                u, b, a = b, b % 2, 1 - b % 2
                if has(0):
                    if at(n, EARLY):
                        pe.wait_ge(acc_done, HALF)
                    pe.wait_ge(xs_in[u // 2], (n - u) * 4 + 16)
                    wait_from(pe, xsT_ready, n)
                    pe.transpose(row_bank(n)[:, 0, :], xs[:, u, 0:C], ident).then_inc(xsT_done, 1)
                if has(1):
                    if at(n, EARLY + 1):
                        pe.wait_ge(pT_ready, HALF)
                    pe.wait_ge(xsT_ready, n)
                    pe.wait_ge(wl_ready, n)
                    wait_from(pe, hT_ready, n - 2)
                    for f in range(FC):
                        mm = pe.matmul(hidden_bank(n, a, f), wl[:, (u - 1) % RING, f * P:(f + 1) * P], xsT[:, a, :],
                                       start=True, stop=True)
                    mm.then_inc(h_done, 1)
                if has(2):
                    if at(n, EARLY + 2):
                        pe.wait_ge(yT_ready, HALF)
                    pe.wait_ge(hT_ready, n - 1)
                    wait_from(pe, biased, n - 2)
                    for f in range(FC):
                        mm = pe.matmul(result_bank(n)[:, 0, :], hT[:, b, f, :], wl[:, (u - 2) % RING, W_2 + f * C:W_2 + (f + 1) * C],
                                       start=(f == 0), stop=(f == FC - 1))
                    mm.then_inc(yy_done, 1)

            def first_attention(n, b, has):
                if at(n, 0):
                    pe.wait_ge(wT_copied, WT_COPIES)
                attention(n, b, has)

            def experts_between(n, b, has):
                if at(n, 0):
                    pe.wait_ge(prod_done, HALF)
                if at(n, 1):
                    pe.wait_ge(sub_done, HALF)
                if at(n, 2):
                    pe.wait_ge(vbd_ready, HALF)
                experts(n, b, has)

            def second_attention(n, b, has):
                if at(n, HALF + 2):
                    pe.wait_ge(hT_ready, SLOT_TILES)
                if at(n, HALF + 3):
                    pe.wait_ge(xsT_ready, SLOT_TILES)
                    pe.wait_ge(biased, SLOT_TILES)
                attention(n, b, has)

            everything(pe, first_attention, experts_between, second_attention, route_counts)

        @block.scalar
        def _(act):
            for t in range(TILES):
                act.wait_ge(mshift_ready, t // XPART + 1)
                act.activation(xn[:, t, 0:C], acc[:, t, :], ACT.Identity, bias=mshift[:, t:t + 1],
                               scale=rstd[:, t:t + 1]).then_inc(xn_ready, 1)

            act.wait_ge(wT_done, 1)
            for s, to in enumerate((wqk[:, 0, :], wqk[:, 1, :], wv[:, :], wp[:, :])):
                act.copy(to.rearrange("p (a c) -> p a c", a=2), s_ps[:, 2 * s:2 * s + 2, :]).then_inc(wT_copied, 1)
            act.copy(wall[:, :, W_B1:W_2], m_ps[:, 0, 0:E * FC].rearrange("p (e f) -> p e f", e=E)).then_inc(wT_copied, 1)

            def route_exp(k):
                if k == 2:
                    act.wait_ge(gap_ready, 1)
                    act.activation(den[:, :], gap[:, :], ACT.Exp).then_inc(gap_exp, 1)

            def attention(n, b, has):
                b, a = b % 2, 1 - b % 2
                if has(4):
                    act.wait_ge(rT_done, n - 3)
                    wait_from(act, yT_ready, n - 4)
                    act.copy(rT[:, :], m_ps[:, 0, :]).then_inc(rT_ready, 1)
                if has(0):
                    act.wait_ge(rot_done, n + 1)
                    wait_from(act, s_done, n - 1)
                    for g in range(NG):
                        gs = slice(GRP * g, GRP * (g + 1))
                        ins = act.copy(kz[gs, b, g, :], rot[gs, 1, :])
                    ins.then_inc(kz_ready, 1)
                    for j in range(NJ):
                        ins = act.activation(qm[:, b, j, :], rot[:, 0, :], ACT.Copy, scale=kc[:, K_MASK + j:K_MASK + j + 1])
                    ins.then_inc(qm_ready, 1)
                if has(1):
                    wait_from(act, v_done, n - 2)
                    act.copy(xv[:, a, :, :, :],
                             xnT[:, bass.ds((n - 1) * P, P)].rearrange("p (c r t) -> p c r t", c=2, r=1)
                             .to_broadcast([P, 2, 2, CHUNK])).then_inc(xv_ready, 1)
                if has(2):
                    act.wait_ge(v_done, n - 1)
                    wait_from(act, y_done, n - 3)
                    for c in range(2):
                        for r in range(2):
                            rs = slice(CHUNK * r, CHUNK * (r + 1))
                            src = v_ps[rs, c, :].rearrange("p (g r j d) -> p j g r d", g=2, r=2, j=NJ)[:, :, :, r, :]
                            dst = vbd[rs, b, c, :, :].rearrange("p g (j w) -> p j g w", j=NJ)[:, :, :, GRP * r:GRP * r + HD]
                            ins = act.copy(dst, src)
                    ins.then_inc(vbd_ready, 1)
                    act.wait_ge(t_done, n - 1)
                    wait_from(act, y_done, n - 3)
                    act.copy(pT[:, b, :, :], t_ps[:, :, :]).then_inc(pT_ready, 1)
                if has(1):
                    act.wait_ge(sub_done, n)
                    act.activation(pr[:, a, :, :], pr[:, a, :, :], ACT.Exp, scale=SCALE).then_inc(exp_done, 1)

            def experts(n, b, has):
                u, b, a = b, b % 2, 1 - b % 2
                if has(1):
                    act.wait_ge(h_done, n)
                    wait_from(act, yy_done, n - 2)
                    for f in range(FC):
                        ins = act.activation(hT[:, a, f, :], hidden_bank(n, a, f),
                                             ACT.Gelu, bias=wl[:, (u - 1) % RING, W_B1 + f:W_B1 + f + 1])
                    ins.then_inc(hT_ready, 1)
                if has(0):
                    act.wait_ge(xsT_done, n + 1)
                    wait_from(act, ys_ready, n - 3)
                    act.copy(slot_w[:, u:u + 1], xs[:, u, C:ROW]).then_inc(slot_w_ready, 1)
                if has(3):
                    w = (u + 1) % RING
                    act.wait_ge(biased, n - 2)
                    act.wait_ge(slot_w_ready, n - 2)
                    act.activation(ys[:, w, :], ys[:, w, :], ACT.Copy, scale=slot_w[:, w:w + 1]).then_inc(ys_ready, 1)

            act.wait_ge(fills, 3)
            everything(act, attention, experts, attention, route_exp)

        @block.vector
        def _(dve):
            dve.memset(wgate[:, :], 0.0).then_inc(wgate_ready, 1)
            dve.memset(zeros[:, :], 0.0).then_inc(fills, 1)
            dve.memset(kz[:, :, :, :], 0.0).then_inc(fills, 1)
            dve.memset(vbd[:, :, :, :, :], 0.0).then_inc(fills, 1)

            def row_stats(i):
                ts = slice(i * XPART, (i + 1) * XPART)
                dve.wait_ge(x_in[i], 16)
                for t in range(i * XPART, (i + 1) * XPART):
                    dve.bn_stats(stats[:, t, :], acc[:, t, :]).then_inc(stats_done, 1)
                for t in range(i * XPART, (i + 1) * XPART):
                    dve.wait_ge(stats_done, t + 1)
                    dve.bn_aggr(mv[:, t, :], stats[:, t, :]).then_inc(mv_done, 1)
                dve.wait_ge(mv_done, (i + 1) * XPART)
                dve.tensor_scalar(nmean[:, ts], mv[:, ts, 0], -1.0, None, ALU.mult)
                dve.tensor_scalar(var[:, ts], mv[:, ts, 1], EPS, None, ALU.add).then_inc(var_ready, 1)

            def keep_transposes(g):
                dve.wait_ge(xnT_done, g + 1)
                dve.tensor_copy(xnT[:, 4 * g * P:4 * (g + 1) * P].rearrange("p (u t) -> p u t", u=4),
                                t_ps[:, 4 * (g % 2):4 * (g % 2) + 4, :]).then_inc(xnT_ready, 1)

            for i in range(6):
                if i < 4:
                    row_stats(i)
                if i == 1:
                    dve.wait_ge(consts_in, 16)
                    for f in range(2):
                        for c in range(2):
                            src = kc[:, K_COS + f * CHUNK:K_COS + (f + 1) * CHUNK].rearrange("p (a t) -> p a t", a=1)
                            dve.tensor_copy(table[:, 2 * f:2 * f + 2, c * CHUNK:(c + 1) * CHUNK],
                                            src.to_broadcast([P, 2, CHUNK])).then_inc(table_ready, 1)
                if i >= 2:
                    keep_transposes(2 * i - 4)
                    keep_transposes(2 * i - 3)
            dve.wait_ge(gate_in, 32)
            dve.wait_ge(lg_done, TILES // 4)
            dve.tensor_tensor(lg[:, :, :], lg_ps[:, 0:TILES * E].rearrange("p (t e) -> p t e", e=E),
                              gbias[:, :].rearrange("p (a e) -> p a e", a=1).to_broadcast([P, TILES, E]),
                              ALU.add).then_inc(lg_ready, 1)
            steps = [0]

            def needs_all():
                dve.wait_ge(route, steps[0])

            def then_route(ins):
                ins.then_inc(route, 1)
                steps[0] += 1

            def over_e(v):
                return v.rearrange("p (t a) -> p t a", a=1).to_broadcast([P, TILES, E])

            e8 = kc[:, K_E8:K_E8 + E].rearrange("p (a e) -> p a e", a=1).to_broadcast([P, TILES, E])
            total = y_ps[:, 2:4, :].rearrange("p a c -> p (a c)")
            run_e = run[:, :].rearrange("p (e t) -> p e t", e=E)

            def routing():
                dve.wait_ge(lg_ready, 1)
                for k in range(2):
                    if k == 1:
                        needs_all()
                    then_route(dve.tensor_reduce(best[:, k, :], lg[:, :, :], AX.X, ALU.max))
                    yield
                    needs_all()
                    then_route(dve.tensor_tensor(work[:, :, :], lg[:, :, :], over_e(best[:, k, :]), ALU.is_equal))
                    yield
                    needs_all()
                    then_route(dve.tensor_tensor(work[:, :, :], work[:, :, :], e8, ALU.mult))
                    yield
                    needs_all()
                    then_route(dve.tensor_reduce(pick[:, k, :], work[:, :, :], AX.X, ALU.min))
                    yield
                    needs_all()
                    then_route(dve.tensor_tensor(hot[:, k, :, :], e8, over_e(pick[:, k, :]), ALU.is_equal))
                    yield
                    if k == 0:
                        needs_all()
                        then_route(dve.scalar_tensor_tensor(out=lg[:, :, :], in0=hot[:, 0, :, :], scalar=FAR, in1=lg[:, :, :],
                                                            op0=ALU.mult, op1=ALU.add))
                        yield
                needs_all()
                dve.tensor_tensor(gap[:, :], best[:, 1, :], best[:, 0, :], ALU.subtract).then_inc(gap_ready, 1)
                then_route(dve.tensor_tensor(both[:, :, :].rearrange("p e t -> p t e"), hot[:, 0, :, :], hot[:, 1, :, :], ALU.add))
                assert steps[0] == ROUTE_BOTH
                yield

                dve.wait_ge(counted, 1)
                then_route(dve.tensor_copy(place[:, :, :].rearrange("p e t -> p (e t)"), total))
                yield
                needs_all()
                then_route(dve.tensor_tensor_scan(run[:, :], kc[:, K_ONE:K_ONE + 1].to_broadcast([P, E * TILES]),
                                                  place[:, :, :].rearrange("p e t -> p (e t)"), 0.0, ALU.mult, ALU.add))
                yield
                needs_all()
                then_route(dve.tensor_tensor(place[:, :, :], run_e, place[:, :, :], ALU.subtract))
                yield
                needs_all()
                then_route(dve.tensor_tensor(place[:, :, :].rearrange("p e t -> p (e t)"), place[:, :, :].rearrange("p e t -> p (e t)"),
                                             y_ps[:, 0:2, :].rearrange("p a c -> p (a c)"), ALU.add))
                assert steps[0] == ROUTE_READ
                yield

                then_route(dve.tensor_copy(load_e[:, 0:1], run_e[:, 0, TILES - 1:TILES]))
                then_route(dve.tensor_tensor(load_e[:, 1:E], run_e[:, 1:E, TILES - 1], run_e[:, 0:E - 1, TILES - 1], ALU.subtract))
                yield
                needs_all()
                then_route(dve.tensor_tensor(many[:, :, :], load_e[:, :].rearrange("p (e a) -> p e a", a=1).to_broadcast([P, E, TILES]),
                                             kc[:, K_STEP:K_STEP + TILES].rearrange("p (a t) -> p a t", a=1).to_broadcast([P, E, TILES]),
                                             ALU.is_gt))
                yield
                needs_all()
                then_route(dve.tensor_reduce(padded[:, :], many[:, :, :], AX.X, ALU.add))
                yield
                needs_all()
                then_route(dve.tensor_scalar(padded[:, :], padded[:, :], float(P), None, ALU.mult))
                yield
                needs_all()
                then_route(dve.tensor_tensor_scan(ends[:, :], kc[:, K_ONE:K_ONE + 1].to_broadcast([P, E]), padded[:, :], 0.0,
                                                  ALU.mult, ALU.add))
                yield
                needs_all()
                then_route(dve.tensor_tensor(shift[:, :], ends[:, :], padded[:, :], ALU.subtract))
                yield
                needs_all()
                then_route(dve.tensor_tensor(shift[:, :], shift[:, :], run_e[:, :, TILES - 1], ALU.subtract))
                yield
                needs_all()
                then_route(dve.tensor_tensor(shift[:, :], shift[:, :], load_e[:, :], ALU.add))
                yield

                needs_all()
                then_route(dve.tensor_tensor(place[:, :, :], place[:, :, :],
                                             shift[:, :].rearrange("p (e a) -> p e a", a=1).to_broadcast([P, E, TILES]), ALU.add))
                yield
                for k in range(2):
                    needs_all()
                    then_route(dve.tensor_tensor(work[:, :, :], hot[:, k, :, :], place[:, :, :].rearrange("p e t -> p t e"), ALU.mult))
                    yield
                    needs_all()
                    then_route(dve.tensor_reduce(posf[:, k, :], work[:, :, :], AX.X, ALU.add))
                    yield

                dve.wait_ge(gap_exp, 1)
                then_route(dve.tensor_scalar(den1[:, :], den[:, :], 1.0, None, ALU.add))
                yield
                needs_all()
                then_route(dve.reciprocal(xn[:, :, C:ROW], den1[:, :].rearrange("p (t a) -> p t a", a=1)))
                yield
                needs_all()
                then_route(dve.tensor_tensor(wt2[:, :], den[:, :], xn[:, :, C:ROW].rearrange("p t a -> p (t a)"), ALU.mult))
                assert steps[0] == ROUTE_WEIGHTS
                needs_all()
                dve.tensor_copy(pos[:, :, :], posf[:, :, :]).then_inc(pos_ready, 1)

                then_route(dve.tensor_tensor(late[:, :, :],
                                             kc[0:1, K_START:K_START + SLOT_TILES].rearrange("p (t a) -> p t a", a=1).to_broadcast([1, SLOT_TILES, E]),
                                             ends[0:1, :].rearrange("p (a e) -> p a e", a=1).to_broadcast([1, SLOT_TILES, E]), ALU.is_ge))
                yield
                needs_all()
                then_route(dve.tensor_reduce(eidf[:, :], late[:, :, :], AX.X, ALU.add))
                yield
                needs_all()
                then_route(dve.tensor_scalar(eidf[:, :], eidf[:, :], float(E - 1), None, ALU.min))
                yield
                needs_all()
                dve.tensor_copy(eid[:, :], eidf[:, :]).then_inc(eid_ready, 1)
                assert steps[0] == ROUTE_END
                yield

            the_routing = routing()
            SHARES = (ROUTE_BOTH // 2, ROUTE_BOTH - ROUTE_BOTH // 2, 4, 8, 8, ROUTE_END)

            def first_attention(n, b, has):
                left = [SHARES[n] if isinstance(n, int) and n < HEAD else 0]
                if at(n, 0):
                    dve.wait_ge(table_ready, 4)

                def route_one(k):
                    while left[0] > 0:
                        left[0] -= 1
                        if next(the_routing, "end") == "end":
                            left[0] = 0
                        if k < LAST_PART:
                            break

                attention(n, b, has, route_one)

            LAST_PART = 7

            def attention(n, b, has, meanwhile):
                b, a = b % 2, 1 - b % 2
                if has(0):
                    dve.wait_ge(qk_done, n + 1)
                    wait_from(dve, rot_done, n)
                    dve.tensor_tensor(rp[:, 2:4, :], qk_ps[:, 0:2, :], table[:, 2:4, :], ALU.mult).then_inc(sines_done, 1)
                    meanwhile(0)
                    dve.wait_ge(sines_done, n + 1)
                    dve.tensor_tensor(rp[:, 0:2, :], qk_ps[:, 0:2, :], table[:, 0:2, :], ALU.mult).then_inc(prod_done, 1)
                    dve.stream_shuffle(sw[:, :, :], rp[:, 2:4, :], SWAP).then_inc(sw_done, 1)
                meanwhile(1)
                if has(5):
                    dve.wait_ge(o_done, n - 4)
                    if has(4):
                        dve.wait_ge(rT_ready, n - 3)
                    dve.tensor_tensor(acc[:, bass.ds(n - 5, 1), :], acc[:, bass.ds(n - 5, 1), :], m_ps[:, 1:2, :],
                                      ALU.add).then_inc(acc_done, 1)
                if has(0):
                    dve.wait_ge(prod_done, n + 1)
                    dve.wait_ge(sw_done, n + 1)
                    wait_from(dve, kz_ready, n)
                    wait_from(dve, qm_ready, n)
                    dve.tensor_tensor(rot[:, :, :], rp[:, 0:2, :], sw[:, :, :], ALU.add).then_inc(rot_done, 1)
                meanwhile(2)
                if has(4):
                    dve.wait_ge(y_done, n - 3)
                    dve.wait_ge(rT_ready, n - 3)
                    wait_from(dve, o_done, n - 5)
                    for c in range(2):
                        cs = slice(CHUNK * c, CHUNK * (c + 1))
                        ins = dve.tensor_tensor(yT[:, b, cs], y_ps[:, c, cs], rT[:, cs], ALU.mult)
                    ins.then_inc(yT_ready, 1)
                meanwhile(3)
                if has(1):
                    dve.wait_ge(s_done, n)
                    wait_from(dve, sub_done, n - 1)
                    dve.tensor_reduce(mx[:, :], s_ps[:, :, :], AX.X, ALU.max).then_inc(max_done, 1)
                meanwhile(4)
                if has(3):
                    dve.wait_ge(sum_done, n - 2)
                    wait_from(dve, rexp_ready, n - 3)
                    dve.reciprocal(rc[:, :], sm[:, :]).then_inc(rc_done, 1)
                if has(1):
                    dve.wait_ge(max_done, n)
                    wait_from(dve, t_done, n - 2)
                    wait_from(dve, sum_done, n - 2)
                    dve.tensor_tensor(pr[:, a, :, :], s_ps[:, :, :],
                                      mx[:, :].rearrange("p (h a) -> p h a", a=1).to_broadcast([P, NJ * NG, CHUNK]),
                                      ALU.subtract).then_inc(sub_done, 1)
                meanwhile(5)
                if has(3):
                    dve.wait_ge(rc_done, n - 2)
                    wait_from(dve, rT_done, n - 3)
                    dve.tensor_copy(rexp[:, :, :, :].rearrange("p g j d -> p j g d"),
                                    rc[:, :].rearrange("p (j g a) -> p j g a", j=NJ, a=1).to_broadcast([P, NJ, NG, HD])
                                    ).then_inc(rexp_ready, 1)
                meanwhile(6)
                if has(2):
                    dve.wait_ge(exp_done, n - 1)
                    wait_from(dve, rc_done, n - 2)
                    dve.tensor_reduce(sm[:, :], pr[:, b, :, :], AX.X, ALU.add).then_inc(sum_done, 1)
                meanwhile(LAST_PART)

            def attention_and_combine(n, b, has):
                m = n - (5 + HALF)
                def combine(k):
                    pair = acc[:, bass.ds(m * 2, 2), :]
                    dve.wait_ge(gathered[1 - b % 2], (m - (1 - b % 2)) * (PAIR // 2) + PAIR)
                    if k == 0:
                        dve.wait_ge(acc_done, n - 4)
                    else:
                        dve.wait_ge(part_done, m + 1)
                    dve.tensor_tensor(pair, pair, got[k][:, bass.ds(m * 2, 2), :], ALU.add).then_inc(tile_done if k else part_done, 1)

                attention(n, b, has, lambda k: combine(k == 6) if k in (3, 6) and has(5) else None)

            def copy_weights(n, u):
                e = nc.vector.value_load(eid[0:1, bass.ds(n, 1)], min_val=0, max_val=E - 1)
                wait_from(dve, biased, n - 3)
                dve.tensor_copy(wl[:, u:u + 1, :], wall[:, bass.ds(e, 1), :]).then_inc(wl_ready, 1)

            def experts(n, b, has):
                u, b = b, b % 2
                if at(n, 0):
                    copy_weights(0, 0)
                if has(0):
                    dve.wait_ge(xsT_done, n + 1)
                    wait_from(dve, h_done, n - 1)
                    dve.tensor_copy(xsT[:, b, :], row_bank(n)[:, 0, :]).then_inc(xsT_ready, 1)
                if has(-1):
                    copy_weights(n + 1, (u + 1) % RING)
                if has(2):
                    dve.wait_ge(yy_done, n - 1)
                    w = (u + 2) % RING
                    wait_from(dve, ys_out[w // 2], (n - (2 + w)) * 4)
                    dve.tensor_tensor(ys[:, w, :], result_bank(n)[:, 0, :], wl[:, w, W_B2:W_B2 + C], ALU.add).then_inc(biased, 1)

            def experts_between(n, b, has):
                if at(n, 0):
                    dve.wait_ge(wall_in, 16 * (E + 2))
                    dve.wait_ge(wT_copied, WT_COPIES)
                    dve.wait_ge(eid_ready, 1)
                experts(n, b, has)

            everything(dve, first_attention, experts_between, attention_and_combine, lambda k: None)


ROUTE_BOTH = 12
ROUTE_READ = ROUTE_BOTH + 4
ROUTE_WEIGHTS = ROUTE_READ + 9 + 5 + 3
ROUTE_END = ROUTE_WEIGHTS + 3
WT_COPIES = 5

_INS = ["L0_attn_x", "L0_attn_w_attn", "L0_attn_w_proj", "L0_ffn_gate_w", "L0_ffn_gate_b",
        "L0_ffn_w1", "L0_ffn_b1", "L0_ffn_w2", "L0_ffn_b2"]


def kernel(**inputs):
    import concourse.bacc as bacc
    from concourse.bass_utils import run_bass_kernel_spmd

    nc = bacc.Bacc("TRN2", target_bir_lowering=False, num_devices=1)
    arrays = {"in_" + n: np.ascontiguousarray(inputs[n]) for n in _INS}
    arrays["in_consts"] = constants()
    aps = [nc.dram_tensor(n, a.shape, mybir.dt.from_np(a.dtype), kind="ExternalInput").ap() for n, a in arrays.items()]
    out = nc.dram_tensor("out_0", (BATCH, SEQ, C), F32, kind="ExternalOutput").ap()
    build(nc, *aps, out)
    r = run_bass_kernel_spmd(nc, [arrays], core_ids=[0])
    return r.results[0]["out_0"]
```
